# Optimizing a Trainium2 kernel written in Bass

```python
import numpy as np
import jax
import jax.numpy as jnp

def _softmax(x, axis=-1):
    return jax.nn.softmax(x, axis=axis)

def _gelu(x):
    return jax.nn.gelu(x, approximate=True)

def _silu(x):
    return jax.nn.silu(x)

def _sigmoid(x):
    return jax.nn.sigmoid(x)

def _layernorm(x, axis=-1, eps=1e-05):
    m = jnp.mean(x, axis=axis, keepdims=True)
    v = jnp.var(x, axis=axis, keepdims=True)
    return (x - m) / jnp.sqrt(v + eps)

def _scatter_add(tgt, idx, src, axis=0):
    return tgt.at[idx].add(src)

def _segment_sum(src, seg, n):
    return jax.ops.segment_sum(src, seg, n)
kernel_name = 'mk_xattn_ffn_d1_seqx_r4_0defcc'

def setup_inputs(seed: int=0):
    np.random.seed(seed)
    _w = jnp.asarray

    def _rec_inputs():
        import jax
        import jax.numpy as jnp
        _rk = jax.random.key(seed)
        x = 7.22e-05 + 1 * jax.random.normal(jax.random.fold_in(_rk, 1), (64, 128, 256), jnp.float32)
        _lenS = 128 - jax.random.randint(jax.random.fold_in(_rk, 7), (64,), 0, max(1, 128 // 4) + 1, jnp.int32)
        _lenS2 = 128 - jax.random.randint(jax.random.fold_in(_rk, 8), (64,), 0, max(1, 128 // 4) + 1, jnp.int32)
        _ctx_768P = jax.random.normal(jax.random.fold_in(_rk, 11), (64, 16, 192), jnp.float32)
        _ctx_768c = jax.random.dirichlet(jax.random.fold_in(_rk, 511), 0.3 * jnp.ones((16,), jnp.float32), (64, 128))
        _ctx_768t = jnp.einsum('bsk,bkd->bsd', _ctx_768c, _ctx_768P)
        _ctx_768t = _ctx_768t * jax.lax.rsqrt(jnp.mean(jnp.square(_ctx_768t)) + 1e-12) * 0.953939
        ctx_768 = -0.000191848 + 0.999787 * (_ctx_768t + 0.3 * jax.random.normal(jax.random.fold_in(_rk, 611), (64, 128, 192), jnp.float32))
        return (x, ctx_768)
    x, ctx_768 = _rec_inputs()

    def _L0_xattn_setup():
        import jax, jax.numpy as jnp
        import numpy as np
        HEADS = 16
        DIM_HEAD = 64
        QUERY_DIM = 256
        CONTEXT_DIM = 192
        INNER = HEADS * DIM_HEAD
        SCALE = DIM_HEAD ** (-0.5)
        key = jax.random.key(seed)
        ks = jax.random.split(key, 7)
        B, Sq, Skv = (4, 512, 512)
        x = jax.random.normal(ks[0], (B, Sq, QUERY_DIM), dtype=jnp.float32)
        context = jax.random.normal(ks[1], (B, Skv, CONTEXT_DIM), dtype=jnp.float32)
        w_q = jax.random.normal(ks[2], (QUERY_DIM, INNER), dtype=jnp.float32) / np.sqrt(QUERY_DIM)
        w_k = jax.random.normal(ks[3], (CONTEXT_DIM, INNER), dtype=jnp.float32) / np.sqrt(CONTEXT_DIM)
        w_v = jax.random.normal(ks[4], (CONTEXT_DIM, INNER), dtype=jnp.float32) / np.sqrt(CONTEXT_DIM)
        w_o = jax.random.normal(ks[5], (INNER, QUERY_DIM), dtype=jnp.float32) / np.sqrt(INNER)
        b_o = jax.random.normal(ks[6], (QUERY_DIM,), dtype=jnp.float32) * 0.02
        return {'x': x, 'context': context, 'w_q': w_q, 'w_k': w_k, 'w_v': w_v, 'w_o': w_o, 'b_o': b_o}
    _L0_xattn_all = _L0_xattn_setup()
    _L0_xattn_in = {k: v for k, v in _L0_xattn_all.items() if k in ('w_q', 'w_k', 'w_v', 'w_o', 'b_o')}
    del _L0_xattn_all

    def _L0_ffn_setup():
        import jax, jax.numpy as jnp
        import numpy as np
        B, T, D, H, E = (4, 512, 256, 512, 8)
        TOP_K = int(E * 0.25)
        key = jax.random.key(seed)
        ks = jax.random.split(key, 6)
        x = jax.random.normal(ks[0], (B, T, D), dtype=jnp.float32)
        gate = jax.random.normal(ks[1], (D, E), dtype=jnp.float32)
        W1 = jax.random.normal(ks[2], (E, D, H), dtype=jnp.float32) * D ** (-0.5)
        b1 = jnp.zeros((E, H), dtype=jnp.float32)
        W2 = jax.random.normal(ks[3], (E, H, D), dtype=jnp.float32) * H ** (-0.5)
        b2 = jnp.zeros((E, D), dtype=jnp.float32)
        return {'x': x, 'gate': gate, 'W1': W1, 'b1': b1, 'W2': W2, 'b2': b2}
    _L0_ffn_all = _L0_ffn_setup()
    _L0_ffn_in = {k: v for k, v in _L0_ffn_all.items() if k in ('gate', 'W1', 'b1', 'W2', 'b2')}
    del _L0_ffn_all
    return {'x': x, 'ctx_768': ctx_768, 'L0_xattn_w_q': _L0_xattn_in['w_q'], 'L0_xattn_w_k': _L0_xattn_in['w_k'], 'L0_xattn_w_v': _L0_xattn_in['w_v'], 'L0_xattn_w_o': _L0_xattn_in['w_o'], 'L0_xattn_b_o': _L0_xattn_in['b_o'], 'L0_ffn_gate': _L0_ffn_in['gate'], 'L0_ffn_W1': _L0_ffn_in['W1'], 'L0_ffn_b1': _L0_ffn_in['b1'], 'L0_ffn_W2': _L0_ffn_in['W2'], 'L0_ffn_b2': _L0_ffn_in['b2']}

def reference(x, ctx_768, L0_xattn_w_q, L0_xattn_w_k, L0_xattn_w_v, L0_xattn_w_o, L0_xattn_b_o, L0_ffn_gate, L0_ffn_W1, L0_ffn_b1, L0_ffn_W2, L0_ffn_b2):
    import jax
    import jax.numpy as jnp

    def _L0_xattn_ref(x, context, w_q, w_k, w_v, w_o, b_o):
        import jax, jax.numpy as jnp
        import numpy as np
        HEADS = 16
        DIM_HEAD = 64
        QUERY_DIM = 256
        CONTEXT_DIM = 192
        INNER = HEADS * DIM_HEAD
        SCALE = DIM_HEAD ** (-0.5)
        B, Sq, _ = x.shape
        Skv = context.shape[1]
        q = (x @ w_q).reshape(B, Sq, HEADS, DIM_HEAD).transpose(0, 2, 1, 3)
        k = (context @ w_k).reshape(B, Skv, HEADS, DIM_HEAD).transpose(0, 2, 1, 3)
        v = (context @ w_v).reshape(B, Skv, HEADS, DIM_HEAD).transpose(0, 2, 1, 3)
        sim = jnp.einsum('bhid,bhjd->bhij', q, k) * SCALE
        attn = jax.nn.softmax(sim, axis=-1)
        out = jnp.einsum('bhij,bhjd->bhid', attn, v)
        out = out.transpose(0, 2, 1, 3).reshape(B, Sq, INNER)
        return out @ w_o + b_o

    def _L0_ffn_ref(x, gate, W1, b1, W2, b2):
        import jax, jax.numpy as jnp
        import numpy as np
        B, T, D, H, E = (4, 512, 256, 512, 8)
        TOP_K = int(E * 0.25)
        raw_gate = jax.nn.softmax(jnp.einsum('btd,de->bte', x, gate), axis=-1)
        topk_scores, topk_idx = jax.lax.top_k(raw_gate, TOP_K)
        mask = jax.nn.one_hot(topk_idx, E, dtype=raw_gate.dtype).sum(axis=-2)
        gate_topk = mask * raw_gate
        gate_topk = gate_topk / jnp.maximum(gate_topk.sum(axis=-1, keepdims=True), 1e-12)
        h = jax.nn.relu(jnp.einsum('btd,edh->beth', x, W1) + b1[None, :, None, :])
        expert_out = jnp.einsum('beth,ehd->betd', h, W2) + b2[None, :, None, :]
        out = jnp.einsum('bte,betd->btd', gate_topk, expert_out)
        return out
    x = x + _L0_xattn_ref(_layernorm(x, axis=-1), ctx_768, L0_xattn_w_q, L0_xattn_w_k, L0_xattn_w_v, L0_xattn_w_o, L0_xattn_b_o)
    x = x + _L0_ffn_ref(_layernorm(x, axis=-1), L0_ffn_gate, L0_ffn_W1, L0_ffn_b1, L0_ffn_W2, L0_ffn_b2)
    return x

_drawn_inputs = setup_inputs


def setup_inputs(seed=0):
    import zlib

    import numpy as np

    out = dict(_drawn_inputs(seed))
    spreads = {'L0_ffn_b1': (0.0, 0.1), 'L0_ffn_b2': (0.0, 0.1)}
    factors = {}
    for name, (base, spread) in spreads.items():
        noise = np.random.default_rng([zlib.crc32(name.encode()), seed]).standard_normal(out[name].shape)
        drawn = base * np.exp(spread * noise) if base else spread * noise
        out[name] = jnp.asarray(drawn.astype(out[name].dtype))
    for name, factor in factors.items():
        out[name] = (out[name] * factor).astype(out[name].dtype)
    return out
```

```python
from contextlib import ExitStack

import numpy as np

import concourse.bass as bass
from concourse import mybir

F32, F32R, I32 = mybir.dt.float32, mybir.dt.float32r, mybir.dt.int32
ALU = mybir.AluOpType
ACT = mybir.ActivationFunctionType
AX = mybir.AxisListType

P = 128
HEAD = 64
EPS_LN = 1e-5
GUARD = 1e-12
TOP = 2
BIG = float(1 << 17)
PREV, CUR, NEXT = "prev", "cur", "next"


class Signal:

    def __init__(self, sem, events, pairs):
        self.sem, self.events, self.pairs = sem, events, pairs

    def present(self, it):
        last = {PREV: self.pairs, CUR: self.pairs - 1, NEXT: self.pairs - 2}
        first = {PREV: 1, CUR: 0, NEXT: -1}
        return [name for name, of in self.events if first[of] <= it <= last[of]]

    def before(self, it):
        return sum(len(self.present(j)) for j in range(-1, it))

    def at(self, it, name):
        if isinstance(it, int):
            here = self.present(it)
            return self.before(it) + here.index(name) + 1 if name in here else 0
        names = [n for n, _ in self.events]
        return it * len(names) + (self.before(1) - len(names) + names.index(name) + 1)


def wait(engine, signal, it, name, back=0):
    value = signal.at(it, name)
    if isinstance(value, int):
        value -= back
        if value > 0:
            engine.wait_ge(signal.sem, value)
    else:
        engine.wait_ge(signal.sem, value - back)


def program(nc, x, ctx, w_q, w_k, w_v, w_o, b_o, gate, W1, b1, W2, b2, out):
    tokens, D = x.shape
    C = ctx.shape[1]
    INNER = w_q.shape[1]
    HEADS = INNER // HEAD
    E, _, H = W1.shape
    PAIRS = tokens // (2 * P)
    HALF = HEADS // 2
    CHUNKS = INNER // P
    SCALE = HEAD ** -0.5
    DC = D // P
    HC = H // P
    REGION = tokens + P
    TILES = TOP * tokens // P + E
    ROW = D + 2
    assert C == P + HEAD and D == 2 * P and HEADS == 16 and TILES % 2 == 0 and PAIRS >= 3

    lists = nc.dram_tensor("lists", ((E + 1) * REGION, ROW), F32, kind="Internal").ap()

    A_SLOTS = [
        [("o0", PREV), ("q10", CUR)],
        [("k10", CUR), ("q11", CUR)],
        [("o1", PREV), ("k11", CUR), ("v10", CUR)],
        [("v11", CUR)],
        [("y0", PREV), ("y1", PREV), ("t0", NEXT), ("t1", NEXT)],
        [("q00", NEXT), ("k00", NEXT)],
        [("q01", NEXT), ("k01", NEXT)],
        [("v00", NEXT), ("v01", NEXT)],
    ]
    A_EVENTS = [e for slot in A_SLOTS for e in slot]
    assert len(A_EVENTS) % 2 == 0
    HI_EVENTS = [e for e in A_EVENTS if e[0][0] in "tqk"]
    UNITS = [(f"u{n}", CUR) for n in range(8)]
    LATE = [("u6", PREV), ("u7", PREV)] + [(f"u{n}", CUR) for n in range(6)]

    ex = ExitStack()
    with ex:
        def sem(name):
            return ex.enter_context(nc.semaphore(name))

        def signal(name, events):
            return Signal(sem(name), events, PAIRS)

        psum = [ex.enter_context(nc.psum_tensor(f"bank_{n}", [P, 512], F32))
                for n in ("a0", "a1", "s0", "s1", "t0", "t1", "v", "g")]
        bank_a, bank_s, bank_t, bank_v, bank_g = psum[0:2], psum[2:4], psum[4:6], psum[6], psum[7]

        def sb_in(stack):
            return lambda name, shape, dt=F32: stack.enter_context(nc.sbuf_tensor(name, shape, dt))

        keep = sb_in(ex)
        ident = keep("ident", [P, P])
        before = keep("before", [P, E, E])
        run = keep("run", [P, E])
        region0 = keep("region0", [P, E])
        pad = keep("pad", [P, ROW])

        const = sem("constants")
        made = sem("made")
        with ExitStack() as a:
            sb = sb_in(a)
            upper = sb("upper", [P, P])
            ones = sb("ones", [P, P])
            after = sb("after", [P, E, E])
            eps = sb("eps", [P, 2])
            mhalf = sb("mhalf", [P, 2])
            step_id = sb("step_id", [P, 2])
            token_id = sb("token_id", [P, 2])
            bo = sb("bo", [P, D])
            gate_sb = sb("gate_sb", [P, DC, E])
            raw = sb("raw", [P, 2048])
            wq = [sb(f"wq_{s}", [P, DC, INNER], F32R) for s in "hl"]
            wk = [sb(f"wk_{s}", [P, INNER], F32R) for s in "hl"]
            wv = [sb(f"wv_{s}", [P, INNER], F32R) for s in "hl"]
            wk2 = sb("wk2", [P, INNER], F32R)
            wv2 = sb("wv2", [P, INNER], F32R)
            wo = [sb(f"wo_{s}", [P, CHUNKS, D], F32R) for s in "hl"]

            xin = sb("xin", [P, 2, D])
            cin = sb("cin", [P, 2, 2 * P])
            xres = sb("xres", [P, 2, D])
            xn = sb("xn", [P, 2, D])
            xt = [sb(f"xt_{s}", [P, DC + 2, 2 * P], F32R) for s in "hl"]
            qt = [sb(f"qt_{s}", [P, 2, CHUNKS // 2, 2 * P], F32R) for s in "hl"]
            kt = [sb(f"kt_{s}", [P, 2, 2, CHUNKS // 2, 2, P], F32R) for s in "hl"]
            vv = sb("vv", [P, 2, 2, HALF * HEAD])
            prob = sb("prob", [P, 4, 4, P])
            probt = sb("probt", [P, 2, 4, P])
            ot = [sb(f"ot_{s}", [P, 2, CHUNKS, P], F32R) for s in "hl"]
            x1 = sb("x1", [P, 2, D])
            rows = sb("rows", [P, 2, 2, ROW])
            yt = sb("yt", [P, 2, DC, P])
            low = sb("low", [P, 4, 4])
            total = sb("total", [P, 4, 4])
            inv = sb("inv", [P, 4, 4])
            stats = sb("stats", [P, 2, 2, 6])
            mean_var = sb("mean_var", [P, 2, 2, 2])
            shifted = sb("shifted", [P, 2, 2])
            rstd = sb("rstd", [P, 2, 2])
            small = lambda name, *s, dt=F32: sb(name, [P, 2, *s], dt)
            g_max, g_sum, g_inv = small("g_max"), small("g_sum"), small("g_inv")
            g_dif, g_exp, g_raw = small("g_dif", E), small("g_exp", E), small("g_raw", E)
            g_ge, g_gt = small("g_ge", E, E), small("g_gt", E, E)
            g_gem, g_gtm, g_cmp = small("g_gem", E, E), small("g_gtm", E, E), small("g_cmp", E, E)
            g_rank, g_mask, g_sel = small("g_rank", E), small("g_mask", E), small("g_sel", E)
            g_ssum, g_smax, g_sinv, g_w = small("g_ssum"), small("g_smax"), small("g_sinv"), small("g_w", E)
            p_pos, p_hi, p_lo = small("p_pos", E), small("p_hi", E), small("p_lo", E)
            p_b, p_a = small("p_b"), small("p_a")
            p_ea, p_eb, p_wa, p_wb = small("p_ea", E), small("p_eb", E), small("p_wa", E), small("p_wb", E)
            slot = sb("slot", [P, 2, 2], I32)

            def wide(t, n):
                return t.rearrange("p (m o) -> p m o", o=1).to_broadcast([P, t.shape[1], n])

            w_raw = [sem(f"w_raw{n}") for n in range(2)]
            w_hi, w_lo = sem("w_hi"), sem("w_lo")
            zeroed = sem("zeroed")
            x_in, c_in, r_in, x1_out = sem("x_in"), sem("c_in"), sem("r_in"), sem("x1_out")
            sent = sem("sent")
            a_full, a_done = signal("a_full", A_EVENTS), signal("a_done", A_EVENTS)
            a_hi = signal("a_hi", HI_EVENTS)
            s_full, s_low, s_exp = signal("s_full", UNITS), signal("s_low", UNITS), signal("s_exp", UNITS)
            s_inv, s_norm = signal("s_inv", UNITS), signal("s_norm", UNITS)
            t_full, t_copy = signal("t_full", LATE), signal("t_copy", LATE)
            v_full, v_hi, v_lo = signal("v_full", LATE), signal("v_hi", LATE), signal("v_lo", LATE)
            DVE_STEPS = (
                [("bn2_0", PREV), ("bn2_1", PREV), ("agg2", PREV), ("ln2", PREV)]
                + [(s, PREV) for s in (
                    "g_max", "g_dif", "g_sum", "g_inv", "g_raw", "g_ge", "g_gt", "g_gem", "g_gtm", "g_cmp",
                    "g_rank", "g_mask", "g_sel", "g_ssum", "g_smax", "g_sinv", "g_w",
                    "p_pos", "p_run", "p_hi", "p_lo", "p_b", "p_a", "p_ea", "p_eb", "p_wa", "p_wb",
                    "wa", "wb", "slot_a", "slot_b")])
            dve_step = signal("dve_step", DVE_STEPS)
            ln1_step = signal("ln1_step", [("bn1_0", NEXT), ("bn1_1", NEXT), ("agg1", NEXT), ("ln1", NEXT)])
            pool_step = signal("pool_step", [("shift1", NEXT), ("rstd1", NEXT), ("shift2", PREV), ("rstd2", PREV),
                                             ("twice", PREV), ("ids", PREV), ("next_id", PREV), ("xres", CUR)])
            g_exps = signal("g_exps", [("g_exp", PREV)])
            gated = signal("gated", [("logits", PREV), ("prefix", PREV)])

            WEIGHTS = []
            for c in range(DC):
                WEIGHTS.append((w_q[c * P:(c + 1) * P, :], INNER, wq[0][:, c, :], wq[1][:, c, :], P))
            for w, d in ((w_k, wk), (w_v, wv)):
                WEIGHTS.append((w[0:P, :], INNER, d[0][:, :], d[1][:, :], P))
            for c in range(0, CHUNKS, 4):
                WEIGHTS.append((w_o[c * P:(c + 4) * P, :].rearrange("(c p) d -> p c d", p=P), 4 * D,
                                wo[0][:, c:c + 4, :], wo[1][:, c:c + 4, :], P))
            TAILS = [(w_k, wk2), (w_v, wv2)]
            NW = len(WEIGHTS)

            def raw_of(n, width, parts=P):
                return raw[0:parts, (n % 2) * 1024:(n % 2) * 1024 + width]

            def iterations(engine, body):
                body(-1)
                body(0)
                with engine.Fori(1, PAIRS - 1) as it:
                    body(it)
                body(PAIRS - 1)
                body(PAIRS)

            def has(it, of):
                first, last = {PREV: (1, PAIRS), CUR: (0, PAIRS - 1), NEXT: (-1, PAIRS - 2)}[of]
                return not isinstance(it, int) or first <= it <= last

            def a_bank(it, name):
                here = a_full.present(it) if isinstance(it, int) else [n for n, _ in A_EVENTS]
                return bank_a[here.index(name) % 2]

            block = a.enter_context(nc.Block())

            @block.sync
            def _(sp):
                sp.dma_start(bo[:, :], b_o.rearrange("(o d) -> o d", o=1).to_broadcast([P, D])).then_inc(const, 16)
                sp.dma_start(gate_sb[:, :, :], gate.rearrange("(c p) e -> p c e", p=P)).then_inc(const, 16)
                sp.wait_ge(made, 17)
                sp.dma_start(out[tokens:tokens + P, :], pad[:, 0:D]).then_inc(x1_out, 16)
                for n, (src, width, hi, lo, parts) in enumerate(WEIGHTS):
                    if n >= 2:
                        sp.wait_ge(w_lo, n - 1)
                    dst = raw_of(n, width)
                    if len(src.shape) == 3:
                        dst = dst.rearrange("p (c d) -> p c d", c=4)
                    sp.dma_start(dst, src).then_inc(w_raw[n % 2], 16)
                for m, (w, d) in enumerate(TAILS):
                    n = NW + m
                    sp.wait_ge(w_lo, n - 1)
                    for k in range(2):
                        sp.dma_start(raw[k * HEAD:(k + 1) * HEAD, (n % 2) * 1024:(n % 2) * 1024 + INNER],
                                     w[P:C, :]).then_inc(w_raw[n % 2], 16)

                def body(it):
                    if has(it, NEXT):
                        row = (it + 1) * (2 * P)
                        if not isinstance(it, int) or it >= 0:
                            wait(sp, ln1_step, it - 1, "ln1")
                            wait(sp, a_full, it - 1, "t1")
                        src = x[bass.ds(row, 2 * P), :].rearrange("(b p) d -> p b d", p=P)
                        sp.dma_start(xin[:, :, :], src).then_inc(x_in, 16)
                        cs = ctx[bass.ds(row, 2 * P), :].rearrange("(b p) d -> p b d", p=P)
                        sp.dma_start(cin[:, :, 0:C], cs).then_inc(c_in, 16)
                        sp.dma_start(cin[:, :, C:2 * P], cs[:, :, P:C]).then_inc(c_in, 16)
                    if has(it, PREV):
                        wait(sp, a_done, it, "o1")
                        dst = out[bass.ds((it - 1) * (2 * P), 2 * P), :].rearrange("(b p) d -> p b d", p=P)
                        sp.dma_start(dst, x1[:, :, :]).then_inc(x1_out, 16)
                    if has(it, CUR):
                        src = x[bass.ds(it * (2 * P), 2 * P), :].rearrange("(b p) d -> p b d", p=P)
                        sp.dma_start(xres[:, :, :], src).then_inc(r_in, 16)

                iterations(sp, body)
                sp.wait_ge(x1_out, 16 * (PAIRS + 1))

            @block.gpsimd
            def _(pool):
                pool.memset(ident[:, :], 0.0).then_inc(made, 1)
                pool.memset(upper[:, :], 0.0).then_inc(made, 1)
                pool.memset(ones[:, :], 1.0).then_inc(made, 1)
                pool.memset(before[:, :, :], 0.0).then_inc(made, 1)
                pool.memset(after[:, :, :], 0.0).then_inc(made, 1)
                pool.memset(eps[:, :], EPS_LN).then_inc(made, 1)
                pool.memset(mhalf[:, :], -0.5).then_inc(made, 1)
                pool.memset(step_id[:, :], 2.0 * P).then_inc(made, 1)
                pool.memset(pad[:, 0:ROW - 1], 0.0).then_inc(made, 1)
                pool.iota(token_id[:, :], [[P, 2]], base=0, channel_multiplier=1,
                          allow_small_or_imprecise_dtypes=True).then_inc(made, 1)
                pool.iota(pad[:, ROW - 1:ROW], [[0, 1]], base=tokens, channel_multiplier=1,
                          allow_small_or_imprecise_dtypes=True).then_inc(made, 1)
                pool.iota(run[:, :], [[REGION, E]], base=0, channel_multiplier=0,
                          allow_small_or_imprecise_dtypes=True).then_inc(made, 1)
                pool.iota(region0[:, :], [[REGION, E]], base=0, channel_multiplier=0,
                          allow_small_or_imprecise_dtypes=True).then_inc(made, 1)
                pool.wait_ge(made, 13)
                pool.affine_select(out=ident[:, :], in_=ident[:, :], compare_op=ALU.not_equal, fill=1.0,
                                   base=0, pattern=[[-1, P]], channel_multiplier=1).then_inc(made, 1)
                pool.affine_select(out=upper[:, :], in_=upper[:, :], compare_op=ALU.is_ge, fill=1.0,
                                   base=0, pattern=[[-1, P]], channel_multiplier=1).then_inc(made, 1)
                pool.affine_select(out=before[:, :, :], in_=before[:, :, :], compare_op=ALU.is_ge, fill=1.0,
                                   base=0, pattern=[[-1, E], [1, E]], channel_multiplier=0).then_inc(made, 1)
                pool.affine_select(out=after[:, :, :], in_=after[:, :, :], compare_op=ALU.is_ge, fill=1.0,
                                   base=0, pattern=[[1, E], [-1, E]], channel_multiplier=0).then_inc(made, 1)
                pool.wait_ge(made, 17)

                def rstd_of(it, k):
                    if k == 0:
                        wait(pool, ln1_step, it, "agg1")
                    else:
                        wait(pool, dve_step, it, "agg2")
                    pool.tensor_tensor(shifted[:, k, :], mean_var[:, k, :, 1], eps[:, :],
                                       ALU.add).then_inc(pool_step.sem, 1)
                    wait(pool, pool_step, it, f"shift{k + 1}")
                    pool.tensor_tensor(rstd[:, k, :], shifted[:, k, :], mhalf[:, :],
                                       ALU.pow).then_inc(pool_step.sem, 1)

                def norm(it, n):
                    wait(pool, s_inv, it, f"u{n}")
                    pool.tensor_tensor(prob[:, n % 4, :, :], prob[:, n % 4, :, :], wide(inv[:, n % 4, :], P),
                                       ALU.mult).then_inc(s_norm.sem, 1)

                def body(it):
                    for n in range(8):
                        if n == 2 and has(it, NEXT):
                            rstd_of(it, 0)
                        if n == 3 and has(it, PREV):
                            rstd_of(it, 1)
                        if n == 4 and has(it, PREV):
                            wait(pool, dve_step, it, "ln2")
                            pool.tensor_tensor(rows[:, :, 1, 0:D], rows[:, :, 0, 0:D],
                                               wide(ones[:, 0:2], D), ALU.mult).then_inc(pool_step.sem, 1)
                            pool.tensor_tensor(rows[:, :, :, D + 1], wide(token_id[:, :], 2), wide(ones[:, 0:2], 2),
                                               ALU.mult).then_inc(pool_step.sem, 1)
                        if has(it, CUR):
                            norm(it, n)
                    if has(it, PREV):
                        wait(pool, dve_step, it, "slot_b")
                        wait(pool, pool_step, it, "ids")
                        pool.tensor_tensor(token_id[:, :], token_id[:, :], step_id[:, :],
                                           ALU.add).then_inc(pool_step.sem, 1)
                        for b in range(2):
                            for k in range(2):
                                pool.indirect_dma_start(
                                    lists, bass.IndirectOffsetOnAxis(ap=slot[:, k, b:b + 1], axis=0),
                                    rows[:, b, k, :], None).then_inc(sent, 16)
                    if has(it, CUR):
                        pool.wait_ge(r_in, (it + 1) * 16)
                        pool.tensor_tensor(xres[:, :, :], xres[:, :, :],
                                           bo[:, :].rearrange("p (o d) -> p o d", o=1).to_broadcast([P, 2, D]),
                                           ALU.add).then_inc(pool_step.sem, 1)

                pool.dma_start(lists[E * REGION:E * REGION + P, :], pad[:, :]).then_inc(sent, 16)
                pool.wait_ge(const, 32)
                iterations(pool, body)
                pool.wait_ge(sent, 64 * PAIRS + 16)

            @block.scalar
            def _(act):
                for n, (src, width, hi, lo, parts) in enumerate(WEIGHTS):
                    act.wait_ge(w_raw[n % 2], 16 * (n // 2 + 1))
                    w = raw_of(n, width)
                    if len(src.shape) == 3:
                        w = w.rearrange("p (c d) -> p c d", c=4)
                    act.activation(hi, w, ACT.Copy).then_inc(w_hi, 1)
                for m, (w, d) in enumerate(TAILS):
                    n = NW + m
                    act.wait_ge(w_raw[n % 2], 16 * (n // 2) + 32)
                    act.activation(d[:, :], raw_of(n, INNER), ACT.Copy).then_inc(w_hi, 1)

                def copy_t(it, name, n):
                    wait(act, t_full, it, name)
                    act.activation(probt[:, n % 2, :, :], bank_t[n % 2][:, :].rearrange("p (h q) -> p h q", h=4),
                                   ACT.Copy).then_inc(t_copy.sem, 1)

                def exps(it, n):
                    wait(act, s_low, it, f"u{n}")
                    for h in range(4):
                        e = act.activation(prob[:, n % 4, h, :], bank_s[n % 2][:, h * P:(h + 1) * P], ACT.Exp,
                                           bias=low[:, n % 4, h:h + 1], scale=-1.0,
                                           accum_out=total[:, n % 4, h:h + 1])
                    e.then_inc(s_exp.sem, 1)

                def hi_part(it, name):
                    wait(act, a_full, it, name)
                    src = a_bank(it, name)
                    kind, k = name[0], int(name[-1])
                    if kind == "t":
                        last = act.activation(xt[0][:, :, k * P:(k + 1) * P],
                                              src[:, :].rearrange("p (c t) -> p c t", c=DC + 2), ACT.Copy)
                    elif kind == "q":
                        last = act.activation(qt[0][:, int(name[1]), 2 * k:2 * k + 2, :],
                                              src[:, :].rearrange("p (c t) -> p c t", c=2), ACT.Copy, scale=-SCALE)
                    else:
                        for side in range(2):
                            part = slice(side * HEAD, (side + 1) * HEAD)
                            last = act.activation(
                                kt[0][part, int(name[1]), :, 2 * k:2 * k + 2, side, :],
                                src[part, :].rearrange("p (c b t) -> p b c t", c=2, b=2), ACT.Copy)
                    last.then_inc(a_hi.sem, 1)

                def hi_out(it, name, n):
                    wait(act, v_full, it, name)
                    c = 4 * (n // 4) + 2 * (n % 2)
                    act.activation(ot[0][:, (n % 4) // 2, c:c + 2, :],
                                   bank_v[:, 0:2 * P].rearrange("p (c q) -> p c q", c=2), ACT.Copy).then_inc(v_hi.sem, 1)

                def body(it):
                    for n in range(8):
                        late, of = LATE[n]
                        if has(it, of):
                            copy_t(it, late, (n - 2) % 8)
                        if has(it, CUR):
                            exps(it, n)
                        for name, o in A_SLOTS[n]:
                            if (name, o) in HI_EVENTS and has(it, o):
                                hi_part(it, name)
                        if n == 5 and has(it, PREV):
                            wait(act, dve_step, it, "g_dif")
                            act.activation(g_exp[:, :, :], g_dif[:, :, :], ACT.Exp).then_inc(g_exps.sem, 1)
                        if has(it, of):
                            hi_out(it, late, (n - 2) % 8)

                iterations(act, body)

            @block.vector
            def _(dve):
                for s in range(2):
                    for side in range(2):
                        part = slice((1 - side) * HEAD, (2 - side) * HEAD)
                        dve.memset(kt[s][part, :, :, :, side, :].bitcast(F32), 0.0).then_inc(zeroed, 1)
                for n, (src, width, hi, lo, parts) in enumerate(WEIGHTS):
                    dve.wait_ge(w_hi, n + 1)
                    w = raw_of(n, width)
                    if len(src.shape) == 3:
                        w = w.rearrange("p (c d) -> p c d", c=4)
                    dve.tensor_tensor(lo, w, hi.bitcast(F32), ALU.subtract).then_inc(w_lo, 1)
                for m, (w, d) in enumerate(TAILS):
                    n = NW + m
                    dve.wait_ge(w_hi, n + 1)
                    dve.tensor_tensor(d[HEAD:P, :], raw_of(n, INNER)[HEAD:P, :], d[HEAD:P, :].bitcast(F32),
                                      ALU.subtract).then_inc(w_lo, 1)

                done = dve_step.sem
                steps = (ln1_step.sem, dve_step.sem)

                def after_step(it, name):
                    wait(dve, dve_step, it, name)

                def lowest(it, n):
                    wait(dve, s_full, it, f"u{n}")
                    dve.tensor_reduce(low[:, n % 4, :], bank_s[n % 2][:, :].rearrange("p (h k) -> p h k", h=4),
                                      AX.X, ALU.min).then_inc(s_low.sem, 1)

                def inverse(it, n):
                    wait(dve, s_exp, it, f"u{n}")
                    dve.reciprocal(inv[:, n % 4, :], total[:, n % 4, :]).then_inc(s_inv.sem, 1)

                def second_part(it, name):
                    src = a_bank(it, name)
                    kind, k = name[0], int(name[-1])
                    if (kind in "tqk"):
                        wait(dve, a_hi, it, name)
                    else:
                        wait(dve, a_full, it, name)
                    if kind == "t":
                        last = dve.tensor_tensor(xt[1][:, :, k * P:(k + 1) * P],
                                                 src[:, :].rearrange("p (c t) -> p c t", c=DC + 2),
                                                 xt[0][:, :, k * P:(k + 1) * P].bitcast(F32), ALU.subtract)
                    elif kind == "q":
                        g = int(name[1])
                        last = dve.scalar_tensor_tensor(qt[1][:, g, 2 * k:2 * k + 2, :],
                                                        src[:, :].rearrange("p (c t) -> p c t", c=2), -SCALE,
                                                        qt[0][:, g, 2 * k:2 * k + 2, :].bitcast(F32),
                                                        ALU.mult, ALU.subtract)
                    elif kind == "k":
                        for side in range(2):
                            part = slice(side * HEAD, (side + 1) * HEAD)
                            at = (part, int(name[1]), slice(None), slice(2 * k, 2 * k + 2), side, slice(None))
                            last = dve.tensor_tensor(kt[1][at], src[part, :].rearrange("p (c b t) -> p b c t", c=2, b=2),
                                                     kt[0][at].bitcast(F32), ALU.subtract)
                    elif kind == "v":
                        last = dve.tensor_copy(vv[:, int(name[1]), k, :], src[:, :])
                    elif kind == "o":
                        wait(dve, pool_step, it - 1, "xres")
                        if k == 0:
                            dve.wait_ge(x1_out, it * 16)
                        last = dve.tensor_tensor(x1[:, k, :], src[:, 0:D], xres[:, k, :], ALU.add)
                    else:
                        last = dve.tensor_copy(yt[:, k, :, :], src[:, 0:D].rearrange("p (c t) -> p c t", c=DC))
                    last.then_inc(a_done.sem, 1)

                def low_out(it, name, n):
                    wait(dve, v_hi, it, name)
                    c = 4 * (n // 4) + 2 * (n % 2)
                    dve.tensor_tensor(ot[1][:, (n % 4) // 2, c:c + 2, :],
                                      bank_v[:, 0:2 * P].rearrange("p (c q) -> p c q", c=2),
                                      ot[0][:, (n % 4) // 2, c:c + 2, :].bitcast(F32),
                                      ALU.subtract).then_inc(v_lo.sem, 1)

                def statistics(k, src):
                    for b in range(2):
                        dve.bn_stats(stats[:, k, b, :], src[:, b, :]).then_inc(steps[k], 1)

                def aggregate(k):
                    for b in range(2):
                        last = dve.bn_aggr(mean_var[:, k, b, :], stats[:, k, b, :])
                    last.then_inc(steps[k], 1)

                def normalise(it, k, src, dst):
                    wait(dve, pool_step, it, f"rstd{k + 1}")
                    for b in range(2):
                        last = dve.tensor_scalar(dst[b], src[:, b, :], mean_var[:, k, b, 0:1], rstd[:, k, b:b + 1],
                                                 ALU.subtract, ALU.mult)
                    last.then_inc(steps[k], 1)

                def gate_scores(it):
                    wait(dve, gated, it, "logits")
                    logits = bank_g[:, 0:2 * E].rearrange("p (b e) -> p b e", b=2)
                    dve.tensor_reduce(g_max[:, :], logits, AX.X, ALU.max).then_inc(done, 1)
                    after_step(it, "g_max")
                    dve.tensor_tensor(g_dif[:, :, :], logits, wide(g_max[:, :], E), ALU.subtract).then_inc(done, 1)

                def gate_top(it):
                    wait(dve, g_exps, it, "g_exp")
                    dve.tensor_reduce(g_sum[:, :], g_exp[:, :, :], AX.X, ALU.add).then_inc(done, 1)
                    after_step(it, "g_sum")
                    dve.reciprocal(g_inv[:, :], g_sum[:, :]).then_inc(done, 1)
                    after_step(it, "g_inv")
                    dve.tensor_tensor(g_raw[:, :, :], g_exp[:, :, :], wide(g_inv[:, :], E), ALU.mult).then_inc(done, 1)
                    after_step(it, "g_raw")
                    for b in range(2):
                        other = g_raw[:, b, :].rearrange("p (o f) -> p o f", o=1).to_broadcast([P, E, E])
                        last = dve.tensor_tensor(g_ge[:, b, :, :], other, wide(g_raw[:, b, :], E), ALU.is_ge)
                    last.then_inc(done, 1)
                    for b in range(2):
                        other = g_raw[:, b, :].rearrange("p (o f) -> p o f", o=1).to_broadcast([P, E, E])
                        last = dve.tensor_tensor(g_gt[:, b, :, :], other, wide(g_raw[:, b, :], E), ALU.is_gt)
                    last.then_inc(done, 1)
                    flat = lambda t: t.rearrange("p b e f -> p b (e f)")
                    both = lambda t: t[:, :, :].rearrange("p e f -> p (e f)").rearrange(
                        "p (o m) -> p o m", o=1).to_broadcast([P, 2, E * E])
                    after_step(it, "g_ge")
                    dve.tensor_tensor(flat(g_gem[:, :, :, :]), flat(g_ge[:, :, :, :]), both(before), ALU.mult).then_inc(done, 1)
                    after_step(it, "g_gt")
                    dve.tensor_tensor(flat(g_gtm[:, :, :, :]), flat(g_gt[:, :, :, :]), both(after), ALU.mult).then_inc(done, 1)
                    after_step(it, "g_gtm")
                    dve.tensor_tensor(flat(g_cmp[:, :, :, :]), flat(g_gem[:, :, :, :]), flat(g_gtm[:, :, :, :]),
                                      ALU.add).then_inc(done, 1)
                    after_step(it, "g_cmp")
                    dve.tensor_reduce(g_rank[:, :, :], g_cmp[:, :, :, :], AX.X, ALU.add).then_inc(done, 1)
                    after_step(it, "g_rank")
                    dve.tensor_scalar(g_mask[:, :, :], g_rank[:, :, :], float(TOP), None, ALU.is_lt).then_inc(done, 1)
                    after_step(it, "g_mask")
                    dve.tensor_tensor(g_sel[:, :, :], g_mask[:, :, :], g_raw[:, :, :], ALU.mult).then_inc(done, 1)
                    after_step(it, "g_sel")
                    dve.tensor_reduce(g_ssum[:, :], g_sel[:, :, :], AX.X, ALU.add).then_inc(done, 1)
                    after_step(it, "g_ssum")
                    dve.tensor_scalar(g_smax[:, :], g_ssum[:, :], GUARD, None, ALU.max).then_inc(done, 1)
                    after_step(it, "g_smax")
                    dve.reciprocal(g_sinv[:, :], g_smax[:, :]).then_inc(done, 1)
                    after_step(it, "g_sinv")
                    dve.tensor_tensor(g_w[:, :, :], g_sel[:, :, :], wide(g_sinv[:, :], E), ALU.mult).then_inc(done, 1)

                def slots_of(it):
                    wait(dve, gated, it, "prefix")
                    first = bank_g[:, 2 * E:4 * E].rearrange("p (b e) -> p b e", b=2)
                    base = run[:, :].rearrange("p (o e) -> p o e", o=1).to_broadcast([P, 2, E])
                    dve.tensor_tensor(p_pos[:, :, :], first, base, ALU.add).then_inc(done, 1)
                    after_step(it, "p_pos")
                    dve.tensor_tensor(run[:, :], bank_g[:, 4 * E:5 * E], run[:, :], ALU.add).then_inc(done, 1)
                    dve.tensor_tensor(p_hi[:, :, :], p_pos[:, :, :], g_mask[:, :, :], ALU.mult).then_inc(done, 1)
                    dve.scalar_tensor_tensor(p_lo[:, :, :], p_pos[:, :, :], -BIG, g_mask[:, :, :],
                                             ALU.add, ALU.mult).then_inc(done, 1)
                    after_step(it, "p_hi")
                    dve.tensor_reduce(p_b[:, :], p_hi[:, :, :], AX.X, ALU.max).then_inc(done, 1)
                    after_step(it, "p_lo")
                    dve.tensor_reduce(p_a[:, :], p_lo[:, :, :], AX.X, ALU.min).then_inc(done, 1)
                    after_step(it, "p_a")
                    dve.tensor_tensor(p_ea[:, :, :], p_lo[:, :, :], wide(p_a[:, :], E), ALU.is_equal).then_inc(done, 1)
                    dve.tensor_tensor(p_eb[:, :, :], p_hi[:, :, :], wide(p_b[:, :], E), ALU.is_equal).then_inc(done, 1)
                    after_step(it, "p_eb")
                    dve.tensor_tensor(p_wa[:, :, :], p_ea[:, :, :], g_w[:, :, :], ALU.mult).then_inc(done, 1)
                    dve.tensor_tensor(p_wb[:, :, :], p_eb[:, :, :], g_w[:, :, :], ALU.mult).then_inc(done, 1)
                    after_step(it, "p_wb")
                    dve.tensor_reduce(rows[:, :, 0, D:D + 1], p_wa[:, :, :], AX.X, ALU.add).then_inc(done, 1)
                    dve.tensor_reduce(rows[:, :, 1, D:D + 1], p_wb[:, :, :], AX.X, ALU.add).then_inc(done, 1)
                    dve.tensor_scalar(slot[:, 0, :], p_a[:, :], BIG, None, ALU.add).then_inc(done, 1)
                    dve.tensor_copy(slot[:, 1, :], p_b[:, :]).then_inc(done, 1)

                def body(it):
                    for n in range(8):
                        if has(it, CUR):
                            lowest(it, n)
                        if n == 1 and has(it, NEXT):
                            dve.wait_ge(x_in, (it + 2) * 16)
                            statistics(0, xin)
                        for name, of in A_SLOTS[n]:
                            if has(it, of):
                                second_part(it, name)
                        if n == 2 and has(it, PREV):
                            wait(dve, a_done, it, "o1")
                            statistics(1, x1)
                        if has(it, CUR):
                            if n == 2:
                                if has(it, NEXT):
                                    wait(dve, ln1_step, it, "bn1_1")
                                if has(it, PREV):
                                    after_step(it, "bn2_1")
                            inverse(it, n)
                        elif n == 2:
                            if has(it, NEXT):
                                wait(dve, ln1_step, it, "bn1_1")
                            if has(it, PREV):
                                after_step(it, "bn2_1")
                        if n == 2 and has(it, NEXT):
                            aggregate(0)
                        if n == 2 and has(it, PREV):
                            aggregate(1)
                        if n == 3 and has(it, NEXT):
                            normalise(it, 0, xin, [xn[:, 0, :], xn[:, 1, :]])
                        if n == 3 and has(it, PREV):
                            dve.wait_ge(sent, (it - 1) * 64 + 16)
                            normalise(it, 1, x1, [rows[:, 0, 0, 0:D], rows[:, 1, 0, 0:D]])
                        if n == 5 and has(it, PREV):
                            gate_scores(it)
                        if n == 6 and has(it, PREV):
                            gate_top(it)
                        if n == 7 and has(it, PREV):
                            slots_of(it)
                        late, of = LATE[n]
                        if has(it, of):
                            low_out(it, late, (n - 2) % 8)

                iterations(dve, body)

            @block.tensor
            def _(pe):
                def three(dst, stat, move, start, stop):
                    for m, (s, r) in enumerate(((0, 1), (1, 0), (0, 0))):
                        last = pe.matmul(dst, stat[s], move[r], start=start and m == 0, stop=stop and m == 2)
                    return last

                def transposes(it, name, n):
                    wait(pe, s_norm, it - 1 if n >= 6 else it, name)
                    wait(pe, t_copy, it, name, 2)
                    for h in range(4):
                        last = pe.transpose(bank_t[n % 2][:, h * P:(h + 1) * P], prob[:, n % 4, h, :], ident[:, :])
                    last.then_inc(t_full.sem, 1)

                def scores(it, n):
                    g, b = n // 4, (n % 4) // 2
                    if n % 4 == 0:
                        last_k = f"k{g}1"
                        wait(pe, a_done, it if g else it - 1, last_k)
                    wait(pe, s_exp, it, f"u{n}", 2)
                    for k in range(2):
                        c = 2 * (n % 2) + k
                        last = three(bank_s[n % 2][:, k * 2 * P:(k + 1) * 2 * P],
                                     [qt[s][:, g, c, b * P:(b + 1) * P] for s in range(2)],
                                     [kt[s][:, g, b, c, :, :].rearrange("p s k -> p (s k)") for s in range(2)], True, True)
                    last.then_inc(s_full.sem, 1)

                def values(it, name, n):
                    g, b = n // 4, (n % 4) // 2
                    if g == 0:
                        wait(pe, a_done, it - 1, f"v0{b}")
                    elif n < 6:
                        wait(pe, a_done, it, "v10")
                    else:
                        wait(pe, a_done, it - 1, "t1")
                    wait(pe, t_copy, it, name)
                    wait(pe, v_lo, it, name, 1)
                    for h in range(4):
                        head = 4 * (n % 2) + h
                        side = slice((h % 2) * HEAD, (h % 2 + 1) * HEAD)
                        last = pe.matmul(bank_v[side, (h // 2) * P:(h // 2 + 1) * P],
                                         vv[:, g, b, head * HEAD:(head + 1) * HEAD], probt[:, n % 2, h, :],
                                         start=True, stop=True, skip_group_check=True)
                    last.then_inc(v_full.sem, 1)

                def product(it, name):
                    dst = a_bank(it, name)
                    kind, k = name[0], int(name[-1])
                    wait(pe, a_done, it, name, 2)
                    if kind == "t":
                        wait(pe, ln1_step, it, "ln1")
                        pe.wait_ge(c_in, (it + 2) * 32)
                        for c in range(DC):
                            pe.transpose(dst[:, c * P:(c + 1) * P], xn[:, k, c * P:(c + 1) * P], ident[:, :])
                        for c in range(2):
                            last = pe.transpose(dst[:, (DC + c) * P:(DC + c + 1) * P],
                                                cin[:, k, c * P:(c + 1) * P], ident[:, :])
                    elif kind == "q":
                        g = int(name[1])
                        if k == 0:
                            t_it = it - 1 if g else it
                            wait(pe, a_done, t_it, "t1")
                        for j in range(2):
                            col = slice((4 * g + 2 * k + j) * P, (4 * g + 2 * k + j + 1) * P)
                            for c in range(DC):
                                last = three(dst[:, j * 2 * P:(j + 1) * 2 * P], [wq[s][:, c, col] for s in range(2)],
                                             [xt[s][:, c, :] for s in range(2)], c == 0, c == DC - 1)
                    elif kind == "k":
                        g = int(name[1])
                        for j in range(2):
                            col = slice((4 * g + 2 * k + j) * P, (4 * g + 2 * k + j + 1) * P)
                            o = dst[:, j * 2 * P:(j + 1) * 2 * P]
                            pe.matmul(o, wk2[0:HEAD, col], xt[1][0:HEAD, DC + 1, :], start=True, stop=False)
                            pe.matmul(o, wk2[:, col], xt[0][:, DC + 1, :], start=False, stop=False)
                            last = three(o, [wk[s][:, col] for s in range(2)],
                                         [xt[s][:, DC, :] for s in range(2)], False, True)
                    elif kind == "v":
                        g = int(name[1])
                        col = slice(g * HALF * HEAD, (g + 1) * HALF * HEAD)
                        tok = slice(k * P, (k + 1) * P)
                        pe.matmul(dst[:, :], xt[1][0:HEAD, DC + 1, tok], wv2[0:HEAD, col], start=True, stop=False)
                        pe.matmul(dst[:, :], xt[0][:, DC + 1, tok], wv2[:, col], start=False, stop=False)
                        last = three(dst[:, :], [xt[s][:, DC, tok] for s in range(2)],
                                     [wv[s][:, col] for s in range(2)], False, True)
                    elif kind == "o":
                        wait(pe, v_lo, it - 1 if k == 0 else it, "u5" if k == 0 else "u7")
                        for c in range(CHUNKS):
                            last = three(dst[:, 0:D], [ot[s][:, k, c, :] for s in range(2)],
                                         [wo[s][:, c, :] for s in range(2)], c == 0, c == CHUNKS - 1)
                    else:
                        wait(pe, dve_step, it, "ln2")
                        for c in range(DC):
                            last = pe.transpose(dst[:, c * P:(c + 1) * P], rows[:, k, 0, c * P:(c + 1) * P], ident[:, :])
                    last.then_inc(a_full.sem, 1)

                def logits(it):
                    wait(pe, a_done, it, "y1")
                    for b in range(2):
                        for c in range(DC):
                            last = pe.matmul(bank_g[:, b * E:(b + 1) * E], yt[:, b, c, :], gate_sb[:, c, :],
                                             start=c == 0, stop=c == DC - 1)
                    last.then_inc(gated.sem, 1)

                def prefix(it):
                    wait(pe, dve_step, it, "g_mask")
                    m = [g_mask[:, b, :] for b in range(2)]
                    at = lambda k: bank_g[:, (2 + k) * E:(3 + k) * E]
                    pe.matmul(at(0), upper[:, :], m[0], start=True, stop=True)
                    pe.matmul(at(1), upper[:, :], m[1], start=True, stop=False)
                    pe.matmul(at(1), ones[:, :], m[0], start=False, stop=True)
                    pe.matmul(at(2), ones[:, :], m[0], start=True, stop=False)
                    pe.matmul(at(2), ones[:, :], m[1], start=False, stop=True).then_inc(gated.sem, 1)

                def body(it):
                    for n in range(8):
                        late, of = LATE[n]
                        if has(it, of):
                            transposes(it, late, (n - 2) % 8)
                        if has(it, CUR):
                            scores(it, n)
                        if n == 5 and has(it, PREV):
                            logits(it)
                        if n == 7 and has(it, PREV):
                            prefix(it)
                        for name, o in A_SLOTS[n]:
                            if has(it, o):
                                product(it, name)
                        if has(it, of):
                            values(it, late, (n - 2) % 8)

                pe.wait_ge(const, 32)
                pe.wait_ge(made, 17)
                pe.wait_ge(zeroed, 4)
                pe.wait_ge(w_lo, NW + 2)
                iterations(pe, body)

        with ExitStack() as stack:
            sb = sb_in(stack)
            RAWS = 4
            STEPS = 4
            assert TILES % STEPS == 0
            stage = sb("stage", [P, RAWS, 1024])
            w1 = [sb(f"w1_{s}", [P, DC, E * H], F32R) for s in "hl"]
            w2 = [sb(f"w2_{s}", [P, HC, E * D], F32R) for s in "hl"]
            b1_all = sb("b1_all", [P, E * H])
            b2_all = sb("b2_all", [P, E * D])
            one = lambda name, *shape, dt=F32: sb(name, [1, *shape], dt)
            count = one("count", E)
            up_i, tiles_i = one("up_i", E, dt=I32), one("tiles_i", E, dt=I32)
            tiles_f, ahead, upto, jump = one("tiles_f", E), one("ahead", E), one("upto", E), one("jump", E)
            ahead_m = one("ahead_m", E, E)
            tile_no = one("tile_no", TILES)
            past = one("past", TILES, E)
            past_jump = one("past_jump", TILES, E)
            expert_f, offset_f, row_f, row_c = (one("expert_f", TILES), one("offset_f", TILES),
                                                one("row_f", TILES), one("row_c", TILES))
            expert_of = one("expert_of", TILES, dt=I32)
            row_of = one("row_of", TILES, dt=I32)
            end_of = one("end_of", E, dt=I32)
            xs = sb("xs", [P, STEPS, ROW])
            tag = sb("tag", [P, STEPS, 2])
            number = sb("number", [P, STEPS, 1], I32)
            xst = [sb(f"xst_{s}", [P, 2, DC, P], F32R) for s in "hl"]
            hid = sb("hid", [P, 2, H])
            hidt = [sb(f"hidt_{s}", [P, 2, HC, P], F32R) for s in "hl"]
            ysum = sb("ysum", [P, 2, D])
            yout = sb("yout", [P, 2, D])

            bank_x, bank_h, bank_ht, bank_y = psum[0:2], psum[2:4], psum[4:6], psum[6:8]

            stage_in = [sem(f"stage_in{n}") for n in range(RAWS)]
            stage_hi, stage_lo = sem("stage_hi"), sem("stage_lo")
            bias_in, table, numbered, padded = sem("bias_in"), sem("table"), sem("numbered"), sem("padded")
            x_tile = [sem(f"x_tile{n}") for n in range(STEPS)]
            x_full, x_hi, x_lo, tagged = sem("x_full"), sem("x_hi"), sem("x_lo"), sem("tagged")
            h_full, h_biased = sem("h_full"), sem("h_biased")
            ht_full, ht_hi, ht_lo = sem("ht_full"), sem("ht_hi"), sem("ht_lo")
            y_full, y_biased, y_weighted, added = sem("y_full"), sem("y_biased"), sem("y_weighted"), sem("added")

            def due(engine, s, value):
                if not isinstance(value, int) or value > 0:
                    engine.wait_ge(s, value)

            STAGED = []
            for e in range(0, E, 2):
                for c in range(DC):
                    STAGED.append((W1[e:e + 2, c * P:(c + 1) * P, :].rearrange("e p h -> p e h"),
                                   [w1[s][:, c, e * H:(e + 2) * H] for s in range(2)], 2))
                for k in range(2):
                    at = slice((e + k) * D, (e + k + 1) * D)
                    STAGED.append((W2[e + k, :, :].rearrange("(c p) d -> p c d", p=P),
                                   [w2[s][:, :, at] for s in range(2)], HC))

            def staged(n, parts, dst):
                flat = stage[:, n % RAWS, :]
                return flat.rearrange("p (a b) -> p a b", a=parts) if len(dst.shape) == 3 else flat

            def tiles(engine, body):
                body(0, False)
                with engine.Fori(1, TILES // STEPS - 1) as it:
                    body(it * STEPS, False)
                body(TILES - STEPS, True)

            block = stack.enter_context(nc.Block())

            @block.sync
            def _(sp):
                sp.dma_start(b1_all[:, :], b1.rearrange("e h -> (e h)").rearrange("(o n) -> o n", o=1)
                             .to_broadcast([P, E * H])).then_inc(bias_in, 16)
                sp.dma_start(b2_all[:, :], b2.rearrange("e d -> (e d)").rearrange("(o n) -> o n", o=1)
                             .to_broadcast([P, E * D])).then_inc(bias_in, 16)
                for n, (src, dst, parts) in enumerate(STAGED):
                    due(sp, stage_lo, n - RAWS + 1)
                    sp.dma_start(stage[:, n % RAWS, :].rearrange("p (a b) -> p a b", a=parts),
                                 src).then_inc(stage_in[n % RAWS], 16)
                sp.wait_ge(table, 1)
                for e in range(E):
                    end = sp.value_load(end_of[0:1, e:e + 1], min_val=e * REGION, max_val=e * REGION + tokens)
                    sp.dma_start(lists[bass.ds(end, P), :], pad[:, :]).then_inc(padded, 16)
                sp.wait_ge(padded, 16 * E)

                def body(j0, last):
                    for u in range(STEPS):
                        j = j0 + u
                        due(sp, x_full, j + 1 - STEPS)
                        due(sp, tagged, j + 1 - STEPS)
                        row = sp.value_load(row_of[0:1, bass.ds(j, 1)], min_val=0, max_val=E * REGION)
                        sp.dma_start(xs[:, u, :], lists[bass.ds(row, P), :]).then_inc(x_tile[u], 16)

                tiles(sp, body)

            @block.gpsimd
            def _(pool):
                pool.iota(tile_no[:, :], [[1, TILES]], base=0, channel_multiplier=0,
                          allow_small_or_imprecise_dtypes=True).then_inc(numbered, 1)

                def weigh(j, u):
                    pool.wait_ge(y_biased, j + 1)
                    due(pool, y_weighted, j)
                    due(pool, added, (j - 1) * 16)
                    pool.tensor_tensor(yout[:, u % 2, :], ysum[:, u % 2, :],
                                       tag[:, u, 0:1].to_broadcast([P, D]), ALU.mult).then_inc(y_weighted, 1)

                def add(u):
                    pool.indirect_dma_start(out, bass.IndirectOffsetOnAxis(ap=number[:, u, :], axis=0),
                                            yout[:, u % 2, :], None, compute_op=ALU.add).then_inc(added, 16)

                def body(j0, last):
                    for u in range(STEPS):
                        weigh(j0 + u, u)
                        if u > 0 or not isinstance(j0, int) or j0 > 0:
                            add((u - 1) % STEPS)

                pool.wait_ge(padded, 16 * E)
                tiles(pool, body)
                pool.wait_ge(y_weighted, TILES)
                pool.wait_ge(added, 16 * (TILES - 1))
                add(STEPS - 1)
                pool.wait_ge(added, 16 * TILES)

            @block.scalar
            def _(act):
                for n, (src, dst, parts) in enumerate(STAGED):
                    act.wait_ge(stage_in[n % RAWS], 16 * (n // RAWS + 1))
                    act.activation(dst[0], staged(n, parts, dst[0]), ACT.Copy).then_inc(stage_hi, 1)

                def x_part(j, u):
                    act.wait_ge(x_full, j + 1)
                    act.activation(xst[0][:, u % 2, :, :], bank_x[u % 2][:, 0:D].rearrange("p (c t) -> p c t", c=DC),
                                   ACT.Copy).then_inc(x_hi, 1)

                def h_part(j, u):
                    act.wait_ge(ht_full, j + 1)
                    act.activation(hidt[0][:, u % 2, :, :], bank_ht[u % 2][:, :].rearrange("p (c t) -> p c t", c=HC),
                                   ACT.Relu).then_inc(ht_hi, 1)

                def body(j0, last):
                    if isinstance(j0, int) and j0 == 0:
                        x_part(0, 0)
                        x_part(1, 1)
                    for u in range(STEPS):
                        h_part(j0 + u, u)
                        if not last or u < STEPS - 2:
                            x_part(j0 + u + 2, u + 2)

                tiles(act, body)

            @block.vector
            def _(dve):
                t = iter(range(2, 99))

                def next_step(instruction):
                    instruction.then_inc(table, 1)
                    dve.wait_ge(table, next(t))

                dve.tensor_copy(end_of[:, :], run[0:1, :]).then_inc(table, 1)
                next_step(dve.tensor_tensor(count[:, :], run[0:1, :], region0[0:1, :], ALU.subtract))
                next_step(dve.tensor_scalar(up_i[:, :], count[:, :], float(P - 1), None, ALU.add))
                next_step(dve.tensor_scalar(tiles_i[:, :], up_i[:, :], P.bit_length() - 1, None,
                                            ALU.arith_shift_right))
                next_step(dve.tensor_copy(tiles_f[:, :], tiles_i[:, :]))
                next_step(dve.tensor_tensor(ahead_m[:, :, :], before[0:1, :, :],
                                            tiles_f[:, :].rearrange("p (o f) -> p o f", o=1).to_broadcast([1, E, E]),
                                            ALU.mult))
                next_step(dve.tensor_reduce(ahead[:, :], ahead_m[:, :, :], AX.X, ALU.add))
                next_step(dve.tensor_tensor(upto[:, :], ahead[:, :], tiles_f[:, :], ALU.add))
                next_step(dve.tensor_scalar(jump[:, :], tiles_f[:, :], -float(P), float(REGION), ALU.mult, ALU.add))
                dve.wait_ge(numbered, 1)
                per_tile = lambda v: v.rearrange("p (o e) -> p o e", o=1).to_broadcast([1, TILES, E])
                next_step(dve.tensor_tensor(past[:, :, :], tile_no[:, :].rearrange("p (j o) -> p j o", o=1)
                                            .to_broadcast([1, TILES, E]), per_tile(upto[:, :]), ALU.is_ge))
                next_step(dve.tensor_reduce(expert_f[:, :], past[:, :, :], AX.X, ALU.add))
                next_step(dve.tensor_scalar(expert_of[:, :], expert_f[:, :], float(E - 1), None, ALU.min))
                next_step(dve.tensor_tensor(past_jump[:, :, :], past[:, :, :], per_tile(jump[:, :]), ALU.mult))
                next_step(dve.tensor_reduce(offset_f[:, :], past_jump[:, :, :], AX.X, ALU.add))
                next_step(dve.scalar_tensor_tensor(row_f[:, :], tile_no[:, :], float(P), offset_f[:, :],
                                                   ALU.mult, ALU.add))
                next_step(dve.tensor_scalar(row_c[:, :], row_f[:, :], float(E * REGION), None, ALU.min))
                dve.tensor_copy(row_of[:, :], row_c[:, :]).then_inc(table, 1)

                for n, (src, dst, parts) in enumerate(STAGED):
                    dve.wait_ge(stage_hi, n + 1)
                    dve.tensor_tensor(dst[1], staged(n, parts, dst[1]), dst[0].bitcast(F32),
                                      ALU.subtract).then_inc(stage_lo, 1)

                def expert(j):
                    return dve.value_load(expert_of[0:1, bass.ds(j, 1)], min_val=0, max_val=E - 1)

                def x_part(j, u):
                    dve.wait_ge(x_hi, j + 1)
                    dve.tensor_tensor(xst[1][:, u % 2, :, :], bank_x[u % 2][:, 0:D].rearrange("p (c t) -> p c t", c=DC),
                                      xst[0][:, u % 2, :, :].bitcast(F32), ALU.subtract).then_inc(x_lo, 1)

                def tags(j, u):
                    due(dve, added, (j + 1 - STEPS) * 16)
                    dve.wait_ge(x_full, j + 1)
                    dve.tensor_copy(tag[:, u % STEPS, 0:1], xs[:, u % STEPS, D:D + 1])
                    dve.tensor_copy(number[:, u % STEPS, :], xs[:, u % STEPS, D + 1:D + 2]).then_inc(tagged, 1)

                def bias1(j, u, e):
                    dve.wait_ge(h_full, j + 1)
                    dve.tensor_tensor(hid[:, u % 2, :], bank_h[u % 2][:, :], b1_all[:, bass.ds(e * H, H)],
                                      ALU.add).then_inc(h_biased, 1)

                def h_part(j, u):
                    dve.wait_ge(ht_hi, j + 1)
                    dve.scalar_tensor_tensor(hidt[1][:, u % 2, :, :],
                                             bank_ht[u % 2][:, :].rearrange("p (c t) -> p c t", c=HC), 0.0,
                                             hidt[0][:, u % 2, :, :].bitcast(F32), ALU.max,
                                             ALU.subtract).then_inc(ht_lo, 1)

                def bias2(j, u, e):
                    dve.wait_ge(y_full, j + 1)
                    due(dve, y_weighted, j - 1)
                    dve.tensor_tensor(ysum[:, u % 2, :], bank_y[u % 2][:, 0:D], b2_all[:, bass.ds(e * D, D)],
                                      ALU.add).then_inc(y_biased, 1)

                dve.wait_ge(bias_in, 32)

                def body(j0, last):
                    if isinstance(j0, int) and j0 == 0:
                        dve.wait_ge(table, 17)
                        x_part(0, 0)
                        x_part(1, 1)
                        bias1(0, 0, expert(0))
                    for u in range(STEPS):
                        h_part(j0 + u, u)
                        if not last or u < STEPS - 2:
                            x_part(j0 + u + 2, u + 2)
                        if not last or u < STEPS - 1:
                            bias1(j0 + u + 1, u + 1, expert(j0 + u + 1))
                        tags(j0 + u, u)
                        bias2(j0 + u, u, expert(j0 + u))

                tiles(dve, body)

            @block.tensor
            def _(pe):
                def three(dst, stat, move, start, stop):
                    for m, (s, r) in enumerate(((0, 1), (1, 0), (0, 0))):
                        last = pe.matmul(dst, stat[s], move[r], start=start and m == 0, stop=stop and m == 2)
                    return last

                def expert(j):
                    return pe.value_load(expert_of[0:1, bass.ds(j, 1)], min_val=0, max_val=E - 1)

                def turn_x(j, u):
                    if isinstance(j, int):
                        pe.wait_ge(x_tile[u % STEPS], 16 * (j // STEPS + 1))
                    else:
                        pe.wait_ge(x_tile[u % STEPS], (j - u % STEPS) * (16 // STEPS) + 16)
                    due(pe, x_lo, j - 1)
                    for c in range(DC):
                        last = pe.transpose(bank_x[u % 2][:, c * P:(c + 1) * P], xs[:, u % STEPS, c * P:(c + 1) * P],
                                            ident[:, :])
                    last.then_inc(x_full, 1)

                def up(j, u, e):
                    pe.wait_ge(x_lo, j + 1)
                    due(pe, h_biased, j - 1)
                    for c in range(DC):
                        last = three(bank_h[u % 2][:, :], [xst[s][:, u % 2, c, :] for s in range(2)],
                                     [w1[s][:, c, bass.ds(e * H, H)] for s in range(2)], c == 0, c == DC - 1)
                    last.then_inc(h_full, 1)

                def turn_h(j, u):
                    pe.wait_ge(h_biased, j + 1)
                    due(pe, ht_lo, j - 1)
                    for c in range(HC):
                        last = pe.transpose(bank_ht[u % 2][:, c * P:(c + 1) * P], hid[:, u % 2, c * P:(c + 1) * P],
                                            ident[:, :])
                    last.then_inc(ht_full, 1)

                def down(j, u, e):
                    pe.wait_ge(ht_lo, j + 1)
                    due(pe, y_biased, j - 1)
                    for c in range(HC):
                        last = three(bank_y[u % 2][:, 0:D], [hidt[s][:, u % 2, c, :] for s in range(2)],
                                     [w2[s][:, c, bass.ds(e * D, D)] for s in range(2)], c == 0, c == HC - 1)
                    last.then_inc(y_full, 1)

                def body(j0, last):
                    if isinstance(j0, int) and j0 == 0:
                        turn_x(0, 0)
                        turn_x(1, 1)
                        up(0, 0, expert(0))
                    for u in range(STEPS):
                        turn_h(j0 + u, u)
                        if not last or u < STEPS - 2:
                            turn_x(j0 + u + 2, u + 2)
                        if not last or u < STEPS - 1:
                            up(j0 + u + 1, u + 1, expert(j0 + u + 1))
                        down(j0 + u, u, expert(j0 + u))

                pe.wait_ge(table, 17)
                pe.wait_ge(stage_lo, len(STAGED))
                tiles(pe, body)


def kernel(x, ctx_768, L0_xattn_w_q, L0_xattn_w_k, L0_xattn_w_v, L0_xattn_w_o, L0_xattn_b_o, L0_ffn_gate,
           L0_ffn_W1, L0_ffn_b1, L0_ffn_W2, L0_ffn_b2):
    import concourse.bacc as bacc
    from concourse.bass_utils import run_bass_kernel_spmd

    nc = bacc.Bacc("TRN2", target_bir_lowering=False, num_devices=1)
    B, S, D = x.shape
    given = {
        "x": np.ascontiguousarray(x).reshape(B * S, D),
        "ctx": np.ascontiguousarray(ctx_768).reshape(B * S, -1),
        "w_q": L0_xattn_w_q, "w_k": L0_xattn_w_k, "w_v": L0_xattn_w_v, "w_o": L0_xattn_w_o, "b_o": L0_xattn_b_o,
        "gate": L0_ffn_gate, "W1": L0_ffn_W1, "b1": L0_ffn_b1, "W2": L0_ffn_W2, "b2": L0_ffn_b2,
    }
    arrays = {f"in_{k}": np.ascontiguousarray(v) for k, v in given.items()}
    aps = [nc.dram_tensor(k, a.shape, mybir.dt.from_np(a.dtype), kind="ExternalInput").ap() for k, a in arrays.items()]
    out = nc.dram_tensor("out", (B * S + P, D), F32, kind="ExternalOutput").ap()
    program(nc, *aps, out)
    r = run_bass_kernel_spmd(nc, [arrays], core_ids=[0])
    return r.results[0]["out"][:B * S].reshape(B, S, D)
```

```python
from contextlib import ExitStack

import numpy as np

import concourse.bass as bass
from concourse import mybir

F32, F32R, I32, BF16 = mybir.dt.float32, mybir.dt.float32r, mybir.dt.int32, mybir.dt.bfloat16
ALU = mybir.AluOpType
ACT = mybir.ActivationFunctionType
AX = mybir.AxisListType

P = 128
HEAD = 64
EPS_LN = 1e-5
GUARD = 1e-12
TOP = 2
BIG = float(1 << 17)
EARLIER, PREV, CUR, NEXT = "earlier", "prev", "cur", "next"


class Signal:

    def __init__(self, sem, events, pairs):
        self.sem, self.events, self.pairs = sem, events, pairs

    def present(self, it):
        last = {EARLIER: self.pairs + 1, PREV: self.pairs, CUR: self.pairs - 1, NEXT: self.pairs - 2}
        first = {EARLIER: 2, PREV: 1, CUR: 0, NEXT: -1}
        return [name for name, of in self.events if first[of] <= it <= last[of]]

    def before(self, it):
        return sum(len(self.present(j)) for j in range(-1, it))

    def at(self, it, name):
        if isinstance(it, int):
            here = self.present(it)
            return self.before(it) + here.index(name) + 1 if name in here else 0
        names = [n for n, _ in self.events]
        return it * len(names) + (self.before(2) - 2 * len(names) + names.index(name) + 1)


def wait(engine, signal, it, name, back=0):
    value = signal.at(it, name)
    if isinstance(value, int):
        value -= back
        if value > 0:
            engine.wait_ge(signal.sem, value)
    else:
        engine.wait_ge(signal.sem, value - back)


def program(nc, x, ctx, w_q, w_k, w_v, w_o, b_o, gate, W1, b1, W2, b2, out):
    tokens, D = x.shape
    C = ctx.shape[1]
    INNER = w_q.shape[1]
    HEADS = INNER // HEAD
    E, _, H = W1.shape
    PAIRS = tokens // (2 * P)
    HALF = HEADS // 2
    CHUNKS = INNER // P
    SCALE = HEAD ** -0.5
    DC = D // P
    HC = H // P
    REGION = tokens + P
    TILES = TOP * tokens // P + E
    ROW = D + 2
    assert C == P + HEAD and D == 2 * P and HEADS == 16 and TILES % 2 == 0 and PAIRS >= 4

    lists = nc.dram_tensor("lists", ((E + 1) * REGION, ROW), F32, kind="Internal").ap()

    A_SLOTS = [
        [("v00", CUR), ("o0", PREV)],
        [("q10", CUR), ("k10", CUR)],
        [("v01", CUR), ("o1", PREV), ("f0", EARLIER), ("f1", EARLIER)],
        [("q11", CUR), ("k11", CUR), ("v10", CUR)],
        [("v11", CUR), ("t0", NEXT), ("t1", NEXT)],
        [("y0", PREV), ("y1", PREV), ("q00", NEXT)],
        [("k00", NEXT), ("q01", NEXT), ("l0", PREV)],
        [("k01", NEXT)],
    ]
    A_EVENTS = [e for slot in A_SLOTS for e in slot]
    A_BANKS = 3
    assert len(A_EVENTS) % A_BANKS == 0
    HI_EVENTS = [e for e in A_EVENTS if e[0][0] in "tqk"]
    UNITS = [(f"u{n}", CUR) for n in range(8)]
    LATE = [("u6", PREV), ("u7", PREV)] + [(f"u{n}", CUR) for n in range(6)]
    NEAR = [("u7", PREV)] + [(f"u{n}", CUR) for n in range(7)]
    LAST = [("u5", PREV), ("u6", PREV), ("u7", PREV)] + [(f"u{n}", CUR) for n in range(5)]

    ex = ExitStack()
    with ex:
        def sem(name):
            return ex.enter_context(nc.semaphore(name))

        def signal(name, events):
            return Signal(sem(name), events, PAIRS)

        psum = [ex.enter_context(nc.psum_tensor(f"bank_{n}", [P, 512], F32))
                for n in ("a0", "a1", "a2", "s0", "s1", "t0", "t1", "v")]
        bank_a, bank_s, bank_t, bank_v = psum[0:3], psum[3:5], psum[5:7], psum[7]

        def sb_in(stack):
            return lambda name, shape, dt=F32: stack.enter_context(nc.sbuf_tensor(name, shape, dt))

        keep = sb_in(ex)
        ident = keep("ident", [P, P])
        before = keep("before", [P, E, E])
        run = keep("run", [P, E])
        region0 = keep("region0", [P, E])
        RAWS = 5
        stage = keep("stage", [P, RAWS, 1024])
        pad = keep("pad", [P, ROW])

        STAGED = []
        for e in range(E):
            STAGED.append((W1[e, :, :].rearrange("(c p) h -> p c h", p=P), (0, e), DC))
            STAGED.append((W2[e, :, :].rearrange("(c p) d -> p c d", p=P), (1, e), HC))

        def staged(n, parts):
            return stage[:, n % RAWS, :].rearrange("p (a b) -> p a b", a=parts)

        stage_in = [sem(f"stage_in{n}") for n in range(RAWS)]

        const = sem("constants")
        made = sem("made")
        with ExitStack() as a:
            sb = sb_in(a)
            upper = sb("upper", [P, P], BF16)
            all_ones = sb("all_ones", [P, P], BF16)
            ones = sb("ones", [P, 2])
            after = sb("after", [P, E, E])
            eps = sb("eps", [P, 2])
            mhalf = sb("mhalf", [P, 2])
            step_id = sb("step_id", [P, 2])
            token_id = sb("token_id", [P, 2])
            bo = sb("bo", [P, D])
            gate_sb = sb("gate_sb", [P, DC, E])
            wq = [sb(f"wq_{s}", [P, DC, INNER], F32R) for s in "hl"]
            wk = [sb(f"wk_{s}", [P, INNER], F32R) for s in "hl"]
            wv = [sb(f"wv_{s}", [P, INNER], F32R) for s in "hl"]
            wk2 = sb("wk2", [P, INNER], F32R)
            wv2 = sb("wv2", [P, INNER], F32R)
            wo = [sb(f"wo_{s}", [P, CHUNKS, D], F32R) for s in "hl"]

            xin = sb("xin", [P, 2, D])
            cin = sb("cin", [P, 2, 2 * P])
            xres = sb("xres", [P, 2, D])
            xn = sb("xn", [P, 2, D])
            xt = [sb(f"xt_{s}", [P, DC + 2, 2 * P], F32R) for s in "hl"]
            qt = [sb(f"qt_{s}", [P, 2, CHUNKS // 2, 2 * P], F32R) for s in "hl"]
            kt = [sb(f"kt_{s}", [P, 2, 2, CHUNKS // 2, 2, P], F32R) for s in "hl"]
            vv = sb("vv", [P, 2, 2, HALF * HEAD])
            prob = sb("prob", [P, 4, 4, P])
            probt = sb("probt", [P, 2, 4, P])
            ot = [sb(f"ot_{s}", [P, 2, CHUNKS, P], F32R) for s in "hl"]
            x1 = sb("x1", [P, 2, D])
            rows = sb("rows", [P, 2, 2, ROW])
            xn2 = sb("xn2", [P, 2, D])
            yt = sb("yt", [P, 2, DC, P])
            low = sb("low", [P, 4, 4])
            total = sb("total", [P, 4, 4])
            inv = sb("inv", [P, 4, 4])
            stats = sb("stats", [P, 2, 2, 6])
            mean_var = sb("mean_var", [P, 2, 2, 2])
            shifted = sb("shifted", [P, 2, 2])
            rstd = sb("rstd", [P, 2, 2])
            small = lambda name, *s, dt=F32: sb(name, [P, 2, *s], dt)
            g_max, g_sum, g_inv = small("g_max"), small("g_sum"), small("g_inv")
            g_log = small("g_log", E)
            g_dif, g_exp, g_raw = small("g_dif", E), small("g_exp", E), small("g_raw", E)
            g_ge, g_gt = small("g_ge", E, E), small("g_gt", E, E)
            g_gem, g_gtm, g_cmp = small("g_gem", E, E), small("g_gtm", E, E), small("g_cmp", E, E)
            g_rank, g_sel = small("g_rank", E), small("g_sel", E)
            g_mask = small("g_mask", E, dt=BF16)
            g_ssum, g_smax, g_sinv, g_w = small("g_ssum"), small("g_smax"), small("g_sinv"), small("g_w", E)
            p_pos, p_hi, p_lo = small("p_pos", E), small("p_hi", E), small("p_lo", E)
            p_b, p_a = small("p_b"), small("p_a")
            p_ea, p_eb, p_wa, p_wb = small("p_ea", E), small("p_eb", E), small("p_wa", E), small("p_wb", E)
            spare = sb("spare", [P, 2])
            slot = sb("slot", [P, 2, 2], I32)

            def wide(t, n):
                return t.rearrange("p (m o) -> p m o", o=1).to_broadcast([P, t.shape[1], n])

            w_hi, w_lo = sem("w_hi"), sem("w_lo")
            zeroed = sem("zeroed")
            x_in, c_in, r_in, x1_out = sem("x_in"), sem("c_in"), sem("r_in"), sem("x1_out")
            sent = sem("sent")
            a_full, a_done = signal("a_full", A_EVENTS), signal("a_done", A_EVENTS)
            a_hi = signal("a_hi", HI_EVENTS)
            s_full, s_low, s_exp = signal("s_full", UNITS), signal("s_low", UNITS), signal("s_exp", UNITS)
            s_inv, s_norm = signal("s_inv", NEAR), signal("s_norm", UNITS)
            t_full, t_copy = signal("t_full", LATE), signal("t_copy", LATE)
            v_full, v_hi, v_lo = signal("v_full", LATE), signal("v_hi", LATE), signal("v_lo", LAST)
            dve_step = signal("dve_step", [(s, PREV) for s in (
                "bn2_0", "bn2_1", "agg2", "ln2", "g_max", "g_dif")])
            route_step = signal("route_step", [(s, EARLIER) for s in (
                "g_sum", "g_inv", "g_raw", "g_ge", "g_gt", "g_gem", "g_gtm", "g_cmp", "g_rank", "g_mask",
                "g_sel", "g_ssum", "g_smax", "g_sinv", "g_w", "p_hi", "p_lo", "p_b", "p_a", "p_ea", "p_eb",
                "p_wa", "p_wb", "wa", "wb", "slot_a", "slot_b")])
            ln1_step = signal("ln1_step", [("bn1_0", NEXT), ("bn1_1", NEXT), ("agg1", NEXT), ("ln1", NEXT)])
            pool_step = signal("pool_step", [
                ("first", EARLIER), ("twice", EARLIER), ("ids", EARLIER), ("next_id", EARLIER),
                ("shift1", NEXT), ("rstd1", NEXT), ("shift2", PREV), ("rstd2", PREV), ("xres", CUR)])
            routed = signal("routed", [("routed", EARLIER)])
            g_exps = signal("g_exps", [("g_exp", PREV)])

            WEIGHTS = [([w_q[c * P:(c + 1) * P, :]], wq[0][:, c, :], wq[1][:, c, :]) for c in range(DC)]
            for w, d, d2 in ((w_k, wk, wk2), (w_v, wv, wv2)):
                WEIGHTS.append(([w[0:P, :]], d[0][:, :], d[1][:, :]))
                WEIGHTS.append(([w[P:C, :], w[P:C, :]], d2[:, :], None))
            for c in range(0, CHUNKS, 4):
                WEIGHTS.append(([w_o[c * P:(c + 4) * P, :].rearrange("(c p) d -> p c d", p=P)],
                                wo[0][:, c:c + 4, :], wo[1][:, c:c + 4, :]))
            NW = len(WEIGHTS)
            Q_READY, K_READY, V_READY = DC, DC + 2, DC + 4
            WHEN = {(-1, 4): (0, Q_READY), (-1, 5): (Q_READY, K_READY), (-1, 7): (K_READY, V_READY),
                    (0, 4): (V_READY, NW)}

            assert INNER == 4 * D == 1024
            w_raw = [sem(f"w_raw{n}") for n in range(NW)]
            stage_more = sb("stage_more", [P, NW - RAWS, 1024])

            def raw_of(n, like=None):
                raw = stage[:, n, :] if n < RAWS else stage_more[:, n - RAWS, :]
                return raw.rearrange("p (c d) -> p c d", c=4) if like is not None and len(like.shape) == 3 else raw

            def iterations(engine, body):
                body(-1)
                body(0)
                body(1)
                with engine.Fori(2, PAIRS - 1) as it:
                    body(it)
                body(PAIRS - 1)
                body(PAIRS)
                body(PAIRS + 1)

            def has(it, of):
                first, last = {EARLIER: (2, PAIRS + 1), PREV: (1, PAIRS), CUR: (0, PAIRS - 1), NEXT: (-1, PAIRS - 2)}[of]
                return not isinstance(it, int) or first <= it <= last

            def a_bank(it, name):
                here = a_full.present(it) if isinstance(it, int) else [n for n, _ in A_EVENTS]
                return bank_a[(a_full.before(it if isinstance(it, int) else 2) + here.index(name)) % A_BANKS]

            block = a.enter_context(nc.Block())

            @block.sync
            def _(sp):
                def load_x(it):
                    row = (it + 1) * (2 * P)
                    src = x[bass.ds(row, 2 * P), :].rearrange("(b p) d -> p b d", p=P)
                    sp.dma_start(xin[:, :, :], src).then_inc(x_in, 16)
                    cs = ctx[bass.ds(row, 2 * P), :].rearrange("(b p) d -> p b d", p=P)
                    sp.dma_start(cin[:, :, 0:C], cs).then_inc(c_in, 16)
                    sp.dma_start(cin[:, :, C:2 * P], cs[:, :, P:C]).then_inc(c_in, 16)

                load_x(-1)
                for n, (sources, hi, _) in enumerate(WEIGHTS):
                    rows_each = P // len(sources)
                    for k, src in enumerate(sources):
                        sp.dma_start(raw_of(n, hi)[k * rows_each:(k + 1) * rows_each], src).then_inc(w_raw[n], 16)
                sp.dma_start(bo[:, :], b_o.rearrange("(o d) -> o d", o=1).to_broadcast([P, D])).then_inc(const, 16)
                sp.dma_start(gate_sb[:, :, :], gate.rearrange("(c p) e -> p c e", p=P)).then_inc(const, 16)
                sp.wait_ge(made, 19)
                sp.dma_start(out[tokens:tokens + P, :], pad[:, 0:D]).then_inc(x1_out, 16)

                def body(it):
                    if has(it, NEXT) and not (isinstance(it, int) and it < 0):
                        wait(sp, ln1_step, it - 1, "ln1")
                        wait(sp, a_full, it - 1, "q00")
                        load_x(it)
                    if has(it, PREV):
                        wait(sp, a_done, it, "o1")
                        dst = out[bass.ds((it - 1) * (2 * P), 2 * P), :].rearrange("(b p) d -> p b d", p=P)
                        sp.dma_start(dst, x1[:, :, :]).then_inc(x1_out, 16)
                    if has(it, CUR):
                        src = x[bass.ds(it * (2 * P), 2 * P), :].rearrange("(b p) d -> p b d", p=P)
                        sp.dma_start(xres[:, :, :], src).then_inc(r_in, 16)

                body(-1)
                body(0)
                for n, (src, dst, parts) in enumerate(STAGED[:RAWS]):
                    sp.wait_ge(w_lo, n + 1)
                    sp.dma_start(staged(n, parts), src).then_inc(stage_in[n], 16)
                body(1)
                with sp.Fori(2, PAIRS - 1) as it:
                    body(it)
                body(PAIRS - 1)
                body(PAIRS)
                body(PAIRS + 1)
                sp.wait_ge(x1_out, 16 * (PAIRS + 1))

            @block.gpsimd
            def _(pool):
                pool.memset(ident[:, :], 0.0).then_inc(made, 1)
                pool.memset(upper[:, :], 0.0).then_inc(made, 1)
                pool.memset(ones[:, :], 1.0).then_inc(made, 1)
                pool.memset(all_ones[:, :], 1.0).then_inc(made, 1)
                pool.memset(before[:, :, :], 0.0).then_inc(made, 1)
                pool.memset(after[:, :, :], 0.0).then_inc(made, 1)
                pool.memset(eps[:, :], EPS_LN).then_inc(made, 1)
                pool.memset(mhalf[:, :], -0.5).then_inc(made, 1)
                pool.memset(step_id[:, :], 2.0 * P).then_inc(made, 1)
                pool.memset(spare[:, :], 0.0).then_inc(made, 1)
                pool.memset(pad[:, 0:ROW - 1], 0.0).then_inc(made, 1)
                pool.iota(token_id[:, :], [[P, 2]], base=0, channel_multiplier=1,
                          allow_small_or_imprecise_dtypes=True).then_inc(made, 1)
                pool.iota(pad[:, ROW - 1:ROW], [[0, 1]], base=tokens, channel_multiplier=1,
                          allow_small_or_imprecise_dtypes=True).then_inc(made, 1)
                pool.iota(run[:, :], [[REGION, E]], base=0, channel_multiplier=0,
                          allow_small_or_imprecise_dtypes=True).then_inc(made, 1)
                pool.iota(region0[:, :], [[REGION, E]], base=0, channel_multiplier=0,
                          allow_small_or_imprecise_dtypes=True).then_inc(made, 1)
                pool.wait_ge(made, 15)
                pool.affine_select(out=ident[:, :], in_=ident[:, :], compare_op=ALU.not_equal, fill=1.0,
                                   base=0, pattern=[[-1, P]], channel_multiplier=1).then_inc(made, 1)
                pool.affine_select(out=upper[:, :], in_=upper[:, :], compare_op=ALU.is_ge, fill=1.0,
                                   base=0, pattern=[[-1, P]], channel_multiplier=1).then_inc(made, 1)
                pool.affine_select(out=before[:, :, :], in_=before[:, :, :], compare_op=ALU.is_ge, fill=1.0,
                                   base=0, pattern=[[-1, E], [1, E]], channel_multiplier=0).then_inc(made, 1)
                pool.affine_select(out=after[:, :, :], in_=after[:, :, :], compare_op=ALU.is_ge, fill=1.0,
                                   base=0, pattern=[[1, E], [-1, E]], channel_multiplier=0).then_inc(made, 1)
                pool.wait_ge(made, 19)

                def rstd_of(it, k):
                    if k == 0:
                        wait(pool, ln1_step, it, "agg1")
                    else:
                        wait(pool, dve_step, it, "agg2")
                    pool.tensor_tensor(shifted[:, k, :], mean_var[:, k, :, 1], eps[:, :],
                                       ALU.add).then_inc(pool_step.sem, 1)
                    wait(pool, pool_step, it, f"shift{k + 1}")
                    pool.tensor_tensor(rstd[:, k, :], shifted[:, k, :], mhalf[:, :],
                                       ALU.pow).then_inc(pool_step.sem, 1)

                def norm(it, n):
                    wait(pool, s_inv, it + 1 if n == 7 else it, f"u{n}")
                    pool.tensor_tensor(prob[:, n % 4, :, :], prob[:, n % 4, :, :], wide(inv[:, n % 4, :], P),
                                       ALU.mult).then_inc(s_norm.sem, 1)

                def body(it):
                    for n in range(8):
                        if n == 2 and has(it, NEXT):
                            rstd_of(it, 0)
                            if isinstance(it, int) and it == -1:
                                zero_keys()
                                pool.wait_ge(const, 32)
                        if n == 3 and has(it, PREV):
                            rstd_of(it, 1)
                        if n == 1 and has(it, EARLIER):
                            wait(pool, dve_step, it - 1, "ln2")
                            pool.wait_ge(sent, (it - 2) * 64 + 16)
                            for k in range(2):
                                pool.tensor_tensor(rows[:, :, k, 0:D], xn2[:, :, :], wide(ones[:, :], D),
                                                   ALU.mult).then_inc(pool_step.sem, 1)
                            pool.tensor_tensor(rows[:, :, :, D + 1], wide(token_id[:, :], 2), wide(ones[:, :], 2),
                                               ALU.mult).then_inc(pool_step.sem, 1)
                            wait(pool, pool_step, it, "ids")
                            pool.tensor_tensor(token_id[:, :], token_id[:, :], step_id[:, :],
                                               ALU.add).then_inc(pool_step.sem, 1)
                        if has(it, CUR):
                            norm(it, n)
                        if n == 6 and has(it, EARLIER):
                            wait(pool, route_step, it, "slot_b")
                            wait(pool, pool_step, it, "next_id")
                            pool.tensor_tensor(spare[:, 1:2], spare[:, 0:1], spare[:, 0:1],
                                               ALU.mult).then_inc(routed.sem, 1)
                        if n in (6, 7) and has(it, EARLIER):
                            for k in range(2):
                                pool.indirect_dma_start(
                                    lists, bass.IndirectOffsetOnAxis(ap=slot[:, k, n - 6:n - 5], axis=0),
                                    rows[:, n - 6, k, :], None).then_inc(sent, 16)
                    if has(it, CUR):
                        pool.wait_ge(r_in, (it + 1) * 16)
                        pool.tensor_tensor(xres[:, :, :], xres[:, :, :],
                                           bo[:, :].rearrange("p (o d) -> p o d", o=1).to_broadcast([P, 2, D]),
                                           ALU.add).then_inc(pool_step.sem, 1)

                def zero_keys():
                    wait(pool, pool_step, -1, "rstd1")
                    for side in range(2):
                        part = slice((1 - side) * HEAD, (2 - side) * HEAD)
                        for s in range(2):
                            pool.memset(kt[s][part, :, :, :, side, :].bitcast(F32), 0.0).then_inc(zeroed, 1)
                        pool.wait_ge(zeroed, 2 * (side + 1))

                pool.dma_start(lists[E * REGION:E * REGION + P, :], pad[:, :]).then_inc(sent, 16)
                iterations(pool, body)
                pool.wait_ge(sent, 64 * PAIRS + 16)

            @block.scalar
            def _(act):
                def prepare(first, last):
                    for n in range(first, last):
                        sources, hi, _ = WEIGHTS[n]
                        act.wait_ge(w_raw[n], 16 * len(sources))
                        act.activation(hi, raw_of(n, hi), ACT.Copy).then_inc(w_hi, 1)

                def copy_t(it, name, n):
                    wait(act, t_full, it, name)
                    act.activation(probt[:, n % 2, :, :], bank_t[n % 2][:, :].rearrange("p (h q) -> p h q", h=4),
                                   ACT.Copy).then_inc(t_copy.sem, 1)

                def exps(it, n):
                    wait(act, s_low, it, f"u{n}")
                    for h in range(4):
                        e = act.activation(prob[:, n % 4, h, :], bank_s[n % 2][:, h * P:(h + 1) * P], ACT.Exp,
                                           bias=low[:, n % 4, h:h + 1], scale=-1.0,
                                           accum_out=total[:, n % 4, h:h + 1])
                    e.then_inc(s_exp.sem, 1)

                def hi_part(it, name):
                    wait(act, a_full, it, name)
                    src = a_bank(it, name)
                    kind, k = name[0], int(name[-1])
                    if kind == "t":
                        last = act.activation(xt[0][:, :, k * P:(k + 1) * P],
                                              src[:, :].rearrange("p (c t) -> p c t", c=DC + 2), ACT.Copy)
                    elif kind == "q":
                        last = act.activation(qt[0][:, int(name[1]), 2 * k:2 * k + 2, :],
                                              src[:, :].rearrange("p (c t) -> p c t", c=2), ACT.Copy, scale=-SCALE)
                    else:
                        for side in range(2):
                            part = slice(side * HEAD, (side + 1) * HEAD)
                            last = act.activation(
                                kt[0][part, int(name[1]), :, 2 * k:2 * k + 2, side, :],
                                src[part, :].rearrange("p (c b t) -> p b c t", c=2, b=2), ACT.Copy)
                    last.then_inc(a_hi.sem, 1)

                def hi_out(it, name, n):
                    wait(act, v_full, it, name)
                    c = 4 * (n // 4) + 2 * (n % 2)
                    act.activation(ot[0][:, (n % 4) // 2, c:c + 2, :],
                                   bank_v[:, 0:2 * P].rearrange("p (c q) -> p c q", c=2), ACT.Copy).then_inc(v_hi.sem, 1)

                def body(it):
                    for n in range(8):
                        if isinstance(it, int) and (it, n) in WHEN:
                            prepare(*WHEN[it, n])
                        late, of = LATE[n]
                        if has(it, of):
                            copy_t(it, late, (n - 2) % 8)
                        if has(it, CUR):
                            exps(it, n)
                        for name, o in A_SLOTS[n]:
                            if (name, o) in HI_EVENTS and has(it, o):
                                hi_part(it, name)
                        if has(it, of):
                            hi_out(it, late, (n - 2) % 8)
                        if n == 7 and has(it, PREV):
                            wait(act, dve_step, it, "g_dif")
                            act.activation(g_exp[:, :, :], g_dif[:, :, :], ACT.Exp).then_inc(g_exps.sem, 1)

                iterations(act, body)

            @block.vector
            def _(dve):
                def prepare(first, last):
                    for n in range(first, last):
                        dve.wait_ge(w_hi, n + 1)
                        _, hi, lo = WEIGHTS[n]
                        raw = raw_of(n, hi)
                        if lo is None:
                            raw, hi = raw[HEAD:P], hi[HEAD:P]
                            lo = hi
                        dve.tensor_tensor(lo, raw, hi.bitcast(F32), ALU.subtract).then_inc(w_lo, 1)

                done, routes = dve_step.sem, route_step.sem
                steps = (ln1_step.sem, dve_step.sem)

                def after_step(it, name):
                    wait(dve, dve_step, it, name)

                def lowest(it, n):
                    wait(dve, s_full, it, f"u{n}")
                    dve.tensor_reduce(low[:, n % 4, :], bank_s[n % 2][:, :].rearrange("p (h k) -> p h k", h=4),
                                      AX.X, ALU.min).then_inc(s_low.sem, 1)

                def inverse(it, name, n):
                    wait(dve, s_exp, it - 1 if n == 7 else it, name)
                    dve.reciprocal(inv[:, n % 4, :], total[:, n % 4, :]).then_inc(s_inv.sem, 1)

                def second_part(it, name):
                    src = a_bank(it, name)
                    kind, k = name[0], int(name[-1])
                    if (kind in "tqk"):
                        wait(dve, a_hi, it, name)
                    else:
                        wait(dve, a_full, it, name)
                    if kind == "t":
                        last = dve.tensor_tensor(xt[1][:, :, k * P:(k + 1) * P],
                                                 src[:, :].rearrange("p (c t) -> p c t", c=DC + 2),
                                                 xt[0][:, :, k * P:(k + 1) * P].bitcast(F32), ALU.subtract)
                    elif kind == "q":
                        g = int(name[1])
                        last = dve.scalar_tensor_tensor(qt[1][:, g, 2 * k:2 * k + 2, :],
                                                        src[:, :].rearrange("p (c t) -> p c t", c=2), -SCALE,
                                                        qt[0][:, g, 2 * k:2 * k + 2, :].bitcast(F32),
                                                        ALU.mult, ALU.subtract)
                    elif kind == "k":
                        for side in range(2):
                            part = slice(side * HEAD, (side + 1) * HEAD)
                            at = (part, int(name[1]), slice(None), slice(2 * k, 2 * k + 2), side, slice(None))
                            last = dve.tensor_tensor(kt[1][at], src[part, :].rearrange("p (c b t) -> p b c t", c=2, b=2),
                                                     kt[0][at].bitcast(F32), ALU.subtract)
                    elif kind == "v":
                        last = dve.tensor_copy(vv[:, int(name[1]), k, :], src[:, :])
                    elif kind == "o":
                        wait(dve, pool_step, it - 1, "xres")
                        if k == 0:
                            dve.wait_ge(x1_out, it * 16)
                        last = dve.tensor_tensor(x1[:, k, :], src[:, 0:D], xres[:, k, :], ALU.add)
                    elif kind == "y":
                        last = dve.tensor_copy(yt[:, k, :, :], src[:, 0:D].rearrange("p (c t) -> p c t", c=DC))
                    elif kind == "l":
                        last = dve.tensor_copy(g_log[:, :, :], src[:, 0:2 * E].rearrange("p (b e) -> p b e", b=2))
                    elif k == 0:
                        base = run[:, :].rearrange("p (o e) -> p o e", o=1).to_broadcast([P, 2, E])
                        last = dve.tensor_tensor(p_pos[:, :, :], src[:, 0:2 * E].rearrange("p (b e) -> p b e", b=2),
                                                 base, ALU.add)
                    else:
                        wait(dve, a_done, it, "f0")
                        last = dve.tensor_tensor(run[:, :], src[:, 0:E], run[:, :], ALU.add)
                    last.then_inc(a_done.sem, 1)

                def low_out(it, name, n):
                    wait(dve, v_hi, it - 1 if n == 5 else it, name)
                    c = 4 * (n // 4) + 2 * (n % 2)
                    dve.tensor_tensor(ot[1][:, (n % 4) // 2, c:c + 2, :],
                                      bank_v[:, 0:2 * P].rearrange("p (c q) -> p c q", c=2),
                                      ot[0][:, (n % 4) // 2, c:c + 2, :].bitcast(F32),
                                      ALU.subtract).then_inc(v_lo.sem, 1)

                def statistics(k, src):
                    for b in range(2):
                        dve.bn_stats(stats[:, k, b, :], src[:, b, :]).then_inc(steps[k], 1)

                def aggregate(k):
                    for b in range(2):
                        last = dve.bn_aggr(mean_var[:, k, b, :], stats[:, k, b, :])
                    last.then_inc(steps[k], 1)

                def normalise(it, k, src, dst):
                    wait(dve, pool_step, it, f"rstd{k + 1}")
                    for b in range(2):
                        last = dve.tensor_scalar(dst[b], src[:, b, :], mean_var[:, k, b, 0:1], rstd[:, k, b:b + 1],
                                                 ALU.subtract, ALU.mult)
                    last.then_inc(steps[k], 1)

                def gate_scores(it):
                    wait(dve, a_done, it, "l0")
                    dve.tensor_reduce(g_max[:, :], g_log[:, :, :], AX.X, ALU.max).then_inc(done, 1)
                    after_step(it, "g_max")
                    dve.tensor_tensor(g_dif[:, :, :], g_log[:, :, :], wide(g_max[:, :], E), ALU.subtract).then_inc(done, 1)

                def gate_top(it):
                    wait(dve, g_exps, it - 1, "g_exp")
                    dve.tensor_reduce(g_sum[:, :], g_exp[:, :, :], AX.X, ALU.add).then_inc(routes, 1)
                    wait(dve, route_step, it, "g_sum")
                    dve.reciprocal(g_inv[:, :], g_sum[:, :]).then_inc(routes, 1)
                    wait(dve, route_step, it, "g_inv")
                    dve.tensor_tensor(g_raw[:, :, :], g_exp[:, :, :], wide(g_inv[:, :], E), ALU.mult).then_inc(routes, 1)
                    wait(dve, route_step, it, "g_raw")
                    for b in range(2):
                        other = g_raw[:, b, :].rearrange("p (o f) -> p o f", o=1).to_broadcast([P, E, E])
                        last = dve.tensor_tensor(g_ge[:, b, :, :], other, wide(g_raw[:, b, :], E), ALU.is_ge)
                    last.then_inc(routes, 1)
                    for b in range(2):
                        other = g_raw[:, b, :].rearrange("p (o f) -> p o f", o=1).to_broadcast([P, E, E])
                        last = dve.tensor_tensor(g_gt[:, b, :, :], other, wide(g_raw[:, b, :], E), ALU.is_gt)
                    last.then_inc(routes, 1)
                    flat = lambda t: t.rearrange("p b e f -> p b (e f)")
                    both = lambda t: t[:, :, :].rearrange("p e f -> p (e f)").rearrange(
                        "p (o m) -> p o m", o=1).to_broadcast([P, 2, E * E])
                    wait(dve, route_step, it, "g_ge")
                    dve.tensor_tensor(flat(g_gem[:, :, :, :]), flat(g_ge[:, :, :, :]), both(before), ALU.mult).then_inc(routes, 1)
                    wait(dve, route_step, it, "g_gt")
                    dve.tensor_tensor(flat(g_gtm[:, :, :, :]), flat(g_gt[:, :, :, :]), both(after), ALU.mult).then_inc(routes, 1)
                    wait(dve, route_step, it, "g_gtm")
                    dve.tensor_tensor(flat(g_cmp[:, :, :, :]), flat(g_gem[:, :, :, :]), flat(g_gtm[:, :, :, :]),
                                      ALU.add).then_inc(routes, 1)
                    wait(dve, route_step, it, "g_cmp")
                    dve.tensor_reduce(g_rank[:, :, :], g_cmp[:, :, :, :], AX.X, ALU.add).then_inc(routes, 1)
                    wait(dve, route_step, it, "g_rank")
                    dve.tensor_scalar(g_mask[:, :, :], g_rank[:, :, :], float(TOP), None, ALU.is_lt).then_inc(routes, 1)

                def gate_weights(it):
                    wait(dve, route_step, it, "g_mask")
                    dve.tensor_tensor(g_sel[:, :, :], g_mask[:, :, :], g_raw[:, :, :], ALU.mult).then_inc(routes, 1)
                    wait(dve, route_step, it, "g_sel")
                    dve.tensor_reduce(g_ssum[:, :], g_sel[:, :, :], AX.X, ALU.add).then_inc(routes, 1)
                    wait(dve, route_step, it, "g_ssum")
                    dve.tensor_scalar(g_smax[:, :], g_ssum[:, :], GUARD, None, ALU.max).then_inc(routes, 1)
                    wait(dve, route_step, it, "g_smax")
                    dve.reciprocal(g_sinv[:, :], g_smax[:, :]).then_inc(routes, 1)
                    wait(dve, route_step, it, "g_sinv")
                    dve.tensor_tensor(g_w[:, :, :], g_sel[:, :, :], wide(g_sinv[:, :], E), ALU.mult).then_inc(routes, 1)

                def slots_of(it):
                    wait(dve, a_done, it, "f0")
                    dve.tensor_tensor(p_hi[:, :, :], p_pos[:, :, :], g_mask[:, :, :], ALU.mult).then_inc(routes, 1)
                    dve.scalar_tensor_tensor(p_lo[:, :, :], p_pos[:, :, :], -BIG, g_mask[:, :, :],
                                             ALU.add, ALU.mult).then_inc(routes, 1)
                    wait(dve, route_step, it, "p_hi")
                    dve.tensor_reduce(p_b[:, :], p_hi[:, :, :], AX.X, ALU.max).then_inc(routes, 1)
                    wait(dve, route_step, it, "p_lo")
                    dve.tensor_reduce(p_a[:, :], p_lo[:, :, :], AX.X, ALU.min).then_inc(routes, 1)
                    wait(dve, route_step, it, "p_a")
                    dve.tensor_tensor(p_ea[:, :, :], p_lo[:, :, :], wide(p_a[:, :], E), ALU.is_equal).then_inc(routes, 1)
                    dve.tensor_tensor(p_eb[:, :, :], p_hi[:, :, :], wide(p_b[:, :], E), ALU.is_equal).then_inc(routes, 1)
                    wait(dve, route_step, it, "p_eb")
                    dve.tensor_tensor(p_wa[:, :, :], p_ea[:, :, :], g_w[:, :, :], ALU.mult).then_inc(routes, 1)
                    dve.tensor_tensor(p_wb[:, :, :], p_eb[:, :, :], g_w[:, :, :], ALU.mult).then_inc(routes, 1)
                    wait(dve, route_step, it, "p_wb")
                    wait(dve, pool_step, it, "ids")
                    dve.tensor_reduce(rows[:, :, 0, D:D + 1], p_wa[:, :, :], AX.X, ALU.add).then_inc(routes, 1)
                    dve.tensor_reduce(rows[:, :, 1, D:D + 1], p_wb[:, :, :], AX.X, ALU.add).then_inc(routes, 1)
                    dve.tensor_scalar(slot[:, 0, :], p_a[:, :], BIG, None, ALU.add).then_inc(routes, 1)
                    dve.tensor_copy(slot[:, 1, :], p_b[:, :]).then_inc(routes, 1)

                def body(it):
                    for n in range(8):
                        if isinstance(it, int) and (it, n) in WHEN:
                            prepare(*WHEN[it, n])
                        if has(it, CUR):
                            lowest(it, n)
                        name, of = LAST[n]
                        if has(it, of):
                            low_out(it, name, (n - 3) % 8)
                        if n == 2 and has(it, NEXT):
                            wait(dve, ln1_step, it, "bn1_1")
                        if n == 3 and has(it, PREV):
                            after_step(it, "bn2_1")
                        name, of = NEAR[n]
                        if has(it, of):
                            inverse(it, name, (n - 1) % 8)
                        if n == 2 and has(it, NEXT):
                            aggregate(0)
                        if n == 3 and has(it, PREV):
                            aggregate(1)
                        if n == 1 and has(it, PREV):
                            second_part(it, "o0")
                        if n == 1 and has(it, EARLIER):
                            gate_weights(it)
                        if n == 7 and has(it, PREV):
                            second_part(it, "l0")
                            gate_scores(it)
                        if n == 1 and has(it, NEXT):
                            dve.wait_ge(x_in, (it + 2) * 16)
                            statistics(0, xin)
                        if n == 3 and has(it, NEXT):
                            normalise(it, 0, xin, [xn[:, 0, :], xn[:, 1, :]])
                        if n == 4 and has(it, PREV):
                            wait(dve, pool_step, it, "twice")
                            normalise(it, 1, x1, [xn2[:, 0, :], xn2[:, 1, :]])
                        for name, of in A_SLOTS[n]:
                            if has(it, of) and name not in ("o0", "l0"):
                                second_part(it, name)
                        if n == 2 and has(it, PREV):
                            wait(dve, a_done, it, "o1")
                            statistics(1, x1)
                        if n == 5 and has(it, EARLIER):
                            slots_of(it)
                        if n == 0 and has(it, EARLIER):
                            gate_top(it)

                iterations(dve, body)

            @block.tensor
            def _(pe):
                def three(dst, stat, move, start, stop):
                    for m, (s, r) in enumerate(((0, 1), (1, 0), (0, 0))):
                        last = pe.matmul(dst, stat[s], move[r], start=start and m == 0, stop=stop and m == 2)
                    return last

                def transposes(it, name, n):
                    wait(pe, s_norm, it - 1 if n >= 6 else it, name)
                    wait(pe, t_copy, it, name, 2)
                    for h in range(4):
                        last = pe.transpose(bank_t[n % 2][:, h * P:(h + 1) * P], prob[:, n % 4, h, :], ident[:, :])
                    last.then_inc(t_full.sem, 1)

                def scores(it, n):
                    g, b = n // 4, (n % 4) // 2
                    if n % 4 < 2:
                        wait(pe, a_done, it if g else it - 1, f"k{g}{n % 4}")
                    wait(pe, s_exp, it, f"u{n}", 2)
                    for k in range(2):
                        c = 2 * (n % 2) + k
                        last = three(bank_s[n % 2][:, k * 2 * P:(k + 1) * 2 * P],
                                     [qt[s][:, g, c, b * P:(b + 1) * P] for s in range(2)],
                                     [kt[s][:, g, b, c, :, :].rearrange("p s k -> p (s k)") for s in range(2)], True, True)
                    last.then_inc(s_full.sem, 1)

                def values(it, name, n):
                    g, b = n // 4, (n % 4) // 2
                    if g == 0:
                        wait(pe, a_done, it, f"v0{b}")
                    elif n < 6:
                        wait(pe, a_done, it, "v10")
                    else:
                        wait(pe, a_done, it - 1, "v11")
                    wait(pe, t_copy, it, name)
                    before_it = LAST[(n + 2) % 8][0]
                    wait(pe, v_lo, it, before_it)
                    for h in range(4):
                        head = 4 * (n % 2) + h
                        side = slice((h % 2) * HEAD, (h % 2 + 1) * HEAD)
                        last = pe.matmul(bank_v[side, (h // 2) * P:(h // 2 + 1) * P],
                                         vv[:, g, b, head * HEAD:(head + 1) * HEAD], probt[:, n % 2, h, :],
                                         start=True, stop=True, skip_group_check=True)
                    last.then_inc(v_full.sem, 1)

                def product(it, name):
                    dst = a_bank(it, name)
                    kind, k = name[0], int(name[-1])
                    wait(pe, a_done, it, name, A_BANKS)
                    if kind == "t":
                        wait(pe, ln1_step, it, "ln1")
                        pe.wait_ge(c_in, (it + 2) * 32)
                        for c in range(DC):
                            pe.transpose(dst[:, c * P:(c + 1) * P], xn[:, k, c * P:(c + 1) * P], ident[:, :])
                        for c in range(2):
                            last = pe.transpose(dst[:, (DC + c) * P:(DC + c + 1) * P],
                                                cin[:, k, c * P:(c + 1) * P], ident[:, :])
                    elif kind == "q":
                        g = int(name[1])
                        if k == 0:
                            wait(pe, a_done, it if g == 0 else it - 1, "t1" if g == 0 else "q00")
                        for j in range(2):
                            col = slice((4 * g + 2 * k + j) * P, (4 * g + 2 * k + j + 1) * P)
                            for c in range(DC):
                                last = three(dst[:, j * 2 * P:(j + 1) * 2 * P], [wq[s][:, c, col] for s in range(2)],
                                             [xt[s][:, c, :] for s in range(2)], c == 0, c == DC - 1)
                    elif kind == "k":
                        g = int(name[1])
                        for j in range(2):
                            col = slice((4 * g + 2 * k + j) * P, (4 * g + 2 * k + j + 1) * P)
                            o = dst[:, j * 2 * P:(j + 1) * 2 * P]
                            pe.matmul(o, wk2[0:HEAD, col], xt[1][0:HEAD, DC + 1, :], start=True, stop=False)
                            pe.matmul(o, wk2[:, col], xt[0][:, DC + 1, :], start=False, stop=False)
                            last = three(o, [wk[s][:, col] for s in range(2)],
                                         [xt[s][:, DC, :] for s in range(2)], False, True)
                    elif kind == "v":
                        g = int(name[1])
                        col = slice(g * HALF * HEAD, (g + 1) * HALF * HEAD)
                        tok = slice(k * P, (k + 1) * P)
                        pe.matmul(dst[:, :], xt[1][0:HEAD, DC + 1, tok], wv2[0:HEAD, col], start=True, stop=False)
                        pe.matmul(dst[:, :], xt[0][:, DC + 1, tok], wv2[:, col], start=False, stop=False)
                        last = three(dst[:, :], [xt[s][:, DC, tok] for s in range(2)],
                                     [wv[s][:, col] for s in range(2)], False, True)
                    elif kind == "o":
                        wait(pe, v_lo, it, "u5" if k == 0 else "u7")
                        for c in range(CHUNKS):
                            last = three(dst[:, 0:D], [ot[s][:, k, c, :] for s in range(2)],
                                         [wo[s][:, c, :] for s in range(2)], c == 0, c == CHUNKS - 1)
                    elif kind == "y":
                        wait(pe, dve_step, it, "ln2")
                        for c in range(DC):
                            last = pe.transpose(dst[:, c * P:(c + 1) * P], xn2[:, k, c * P:(c + 1) * P], ident[:, :])
                    elif kind == "l":
                        wait(pe, a_done, it, "y1")
                        for b in range(2):
                            for c in range(DC):
                                last = pe.matmul(dst[:, b * E:(b + 1) * E], yt[:, b, c, :], gate_sb[:, c, :],
                                                 start=c == 0, stop=c == DC - 1)
                    elif k == 0:
                        wait(pe, route_step, it, "g_mask")
                        pe.matmul(dst[:, 0:2 * E], upper[:, :], g_mask[:, :, :].rearrange("p b e -> p (b e)"),
                                  start=True, stop=False, skip_group_check=True)
                        last = pe.matmul(dst[:, E:2 * E], all_ones[:, :], g_mask[:, 0, :], start=False, stop=True,
                                         skip_group_check=True)
                    else:
                        for b in range(2):
                            last = pe.matmul(dst[:, 0:E], all_ones[:, :], g_mask[:, b, :], start=b == 0, stop=b == 1)
                    last.then_inc(a_full.sem, 1)

                def body(it):
                    for n in range(8):
                        if isinstance(it, int) and it == -1 and n == 5:
                            pe.wait_ge(w_lo, Q_READY)
                        if isinstance(it, int) and it == -1 and n == 6:
                            pe.wait_ge(w_lo, K_READY)
                        if isinstance(it, int) and it == 0 and n == 0:
                            pe.wait_ge(w_lo, V_READY)
                            pe.wait_ge(zeroed, 4)
                        if isinstance(it, int) and it == 1 and n == 0:
                            pe.wait_ge(w_lo, NW)
                            pe.wait_ge(const, 32)
                        late, of = LATE[n]
                        if has(it, of):
                            transposes(it, late, (n - 2) % 8)
                        if has(it, CUR):
                            scores(it, n)
                        for name, o in A_SLOTS[n]:
                            if has(it, o):
                                product(it, name)
                        if has(it, of):
                            values(it, late, (n - 2) % 8)

                pe.wait_ge(made, 19)
                iterations(pe, body)

        with ExitStack() as stack:
            sb = sb_in(stack)
            STEPS = 4
            assert TILES % STEPS == 0
            SPAN = DC * H
            assert SPAN == HC * D
            w1 = [sb(f"w1_{s}", [P, E * SPAN], F32R) for s in "hl"]
            w2 = [sb(f"w2_{s}", [P, E * SPAN], F32R) for s in "hl"]
            b1_all = sb("b1_all", [P, E * H])
            b2_all = sb("b2_all", [P, E * D])
            one = lambda name, *shape, dt=F32: sb(name, [1, *shape], dt)
            count = one("count", E)
            up_i, tiles_i = one("up_i", E, dt=I32), one("tiles_i", E, dt=I32)
            tiles_f, ahead, upto, jump = one("tiles_f", E), one("ahead", E), one("upto", E), one("jump", E)
            ahead_m = one("ahead_m", E, E)
            tile_no = one("tile_no", TILES)
            past = one("past", TILES, E)
            expert_f, offset_f, row_f, row_c = (one("expert_f", TILES), one("offset_f", TILES),
                                                one("row_f", TILES), one("row_c", TILES))
            expert_of = one("expert_of", TILES, dt=I32)
            weights_of = one("weights_of", TILES, dt=I32)
            row_of = one("row_of", TILES, dt=I32)
            end_of = one("end_of", E, dt=I32)
            xs = sb("xs", [P, STEPS, ROW])
            tag = sb("tag", [P, STEPS, 2])
            number = sb("number", [P, STEPS, 1], I32)
            xst = [sb(f"xst_{s}", [P, 2, DC, P], F32R) for s in "hl"]
            hid = sb("hid", [P, 2, H])
            hidt = [sb(f"hidt_{s}", [P, 2, HC, P], F32R) for s in "hl"]
            ysum = sb("ysum", [P, 2, D])
            yout = sb("yout", [P, 2, D])

            bank_x, bank_h, bank_ht, bank_y = psum[0:2], psum[2:4], psum[4:6], psum[6:8]

            def part_of(n, s):
                which, e = STAGED[n][1]
                w, parts = (w1, DC) if which == 0 else (w2, HC)
                return w[s][:, e * SPAN:(e + 1) * SPAN].rearrange("p (c n) -> p c n", c=parts)

            stage_hi, stage_lo = sem("stage_hi"), sem("stage_lo")
            bias_in, table, numbered, padded = sem("bias_in"), sem("table"), sem("numbered"), sem("padded")
            x_tile = [sem(f"x_tile{n}") for n in range(STEPS)]
            x_full, x_hi, x_lo, tagged = sem("x_full"), sem("x_hi"), sem("x_lo"), sem("tagged")
            h_full, h_biased = sem("h_full"), sem("h_biased")
            ht_full, ht_hi, ht_lo = sem("ht_full"), sem("ht_hi"), sem("ht_lo")
            y_full, y_biased, y_weighted, added = sem("y_full"), sem("y_biased"), sem("y_weighted"), sem("added")

            def due(engine, s, value):
                if not isinstance(value, int) or value > 0:
                    engine.wait_ge(s, value)

            def tiles(engine, body):
                body(0, False)
                with engine.Fori(1, TILES // STEPS - 1) as it:
                    body(it * STEPS, False)
                body(TILES - STEPS, True)

            block = stack.enter_context(nc.Block())

            @block.sync
            def _(sp):
                sp.dma_start(b1_all[:, :], b1.rearrange("e h -> (e h)").rearrange("(o n) -> o n", o=1)
                             .to_broadcast([P, E * H])).then_inc(bias_in, 16)
                sp.dma_start(b2_all[:, :], b2.rearrange("e d -> (e d)").rearrange("(o n) -> o n", o=1)
                             .to_broadcast([P, E * D])).then_inc(bias_in, 16)
                for n in range(RAWS, len(STAGED)):
                    src, _, parts = STAGED[n]
                    sp.wait_ge(stage_lo, n - RAWS + 1)
                    sp.dma_start(staged(n, parts), src).then_inc(stage_in[n % RAWS], 16)
                sp.wait_ge(table, 1)
                for e in range(E):
                    end = sp.value_load(end_of[0:1, e:e + 1], min_val=e * REGION, max_val=e * REGION + tokens)
                    sp.dma_start(lists[bass.ds(end, P), :], pad[:, :]).then_inc(padded, 16)
                sp.wait_ge(padded, 16 * E)

                def body(j0, last):
                    for u in range(STEPS):
                        j = j0 + u
                        due(sp, x_full, j + 1 - STEPS)
                        due(sp, tagged, j + 1 - STEPS)
                        row = sp.value_load(row_of[0:1, bass.ds(j, 1)], min_val=0, max_val=E * REGION)
                        sp.dma_start(xs[:, u, :], lists[bass.ds(row, P), :]).then_inc(x_tile[u], 16)

                tiles(sp, body)

            @block.gpsimd
            def _(pool):
                pool.iota(tile_no[:, :], [[1, TILES]], base=0, channel_multiplier=0,
                          allow_small_or_imprecise_dtypes=True).then_inc(numbered, 1)

                def weigh(j, u):
                    pool.wait_ge(y_biased, j + 1)
                    due(pool, y_weighted, j)
                    due(pool, added, (j - 1) * 16)
                    pool.tensor_tensor(yout[:, u % 2, :], ysum[:, u % 2, :],
                                       tag[:, u, 0:1].to_broadcast([P, D]), ALU.mult).then_inc(y_weighted, 1)

                def add(u):
                    pool.indirect_dma_start(out, bass.IndirectOffsetOnAxis(ap=number[:, u, :], axis=0),
                                            yout[:, u % 2, :], None, compute_op=ALU.add).then_inc(added, 16)

                def body(j0, last):
                    for u in range(STEPS):
                        weigh(j0 + u, u)
                        if u > 0 or not isinstance(j0, int) or j0 > 0:
                            add((u - 1) % STEPS)

                pool.wait_ge(padded, 16 * E)
                tiles(pool, body)
                pool.wait_ge(y_weighted, TILES)
                pool.wait_ge(added, 16 * (TILES - 1))
                add(STEPS - 1)
                pool.wait_ge(added, 16 * TILES)

            @block.scalar
            def _(act):
                for n, (_, _, parts) in enumerate(STAGED):
                    act.wait_ge(stage_in[n % RAWS], 16 * (n // RAWS + 1))
                    act.activation(part_of(n, 0), staged(n, parts), ACT.Copy).then_inc(stage_hi, 1)

                def x_part(j, u):
                    act.wait_ge(x_full, j + 1)
                    act.activation(xst[0][:, u % 2, :, :], bank_x[u % 2][:, 0:D].rearrange("p (c t) -> p c t", c=DC),
                                   ACT.Copy).then_inc(x_hi, 1)

                def h_part(j, u):
                    act.wait_ge(ht_full, j + 1)
                    act.activation(hidt[0][:, u % 2, :, :], bank_ht[u % 2][:, :].rearrange("p (c t) -> p c t", c=HC),
                                   ACT.Relu).then_inc(ht_hi, 1)

                def body(j0, last):
                    if isinstance(j0, int) and j0 == 0:
                        x_part(0, 0)
                        x_part(1, 1)
                    for u in range(STEPS):
                        h_part(j0 + u, u)
                        if not last or u < STEPS - 2:
                            x_part(j0 + u + 2, u + 2)

                tiles(act, body)

            @block.vector
            def _(dve):
                def split(first, last):
                    for n in range(first, last):
                        dve.wait_ge(stage_hi, n + 1)
                        dve.tensor_tensor(part_of(n, 1), staged(n, STAGED[n][2]), part_of(n, 0).bitcast(F32),
                                          ALU.subtract).then_inc(stage_lo, 1)

                split(0, RAWS)
                t = iter(range(2, 99))

                def next_step(instruction):
                    instruction.then_inc(table, 1)
                    dve.wait_ge(table, next(t))

                dve.tensor_copy(end_of[:, :], run[0:1, :]).then_inc(table, 1)
                next_step(dve.tensor_tensor(count[:, :], run[0:1, :], region0[0:1, :], ALU.subtract))
                next_step(dve.tensor_scalar(up_i[:, :], count[:, :], float(P - 1), None, ALU.add))
                next_step(dve.tensor_scalar(tiles_i[:, :], up_i[:, :], P.bit_length() - 1, None,
                                            ALU.arith_shift_right))
                next_step(dve.tensor_copy(tiles_f[:, :], tiles_i[:, :]))
                next_step(dve.tensor_tensor(ahead_m[:, :, :], before[0:1, :, :],
                                            tiles_f[:, :].rearrange("p (o f) -> p o f", o=1).to_broadcast([1, E, E]),
                                            ALU.mult))
                next_step(dve.tensor_reduce(ahead[:, :], ahead_m[:, :, :], AX.X, ALU.add))
                next_step(dve.tensor_tensor(upto[:, :], ahead[:, :], tiles_f[:, :], ALU.add))
                next_step(dve.tensor_scalar(jump[:, :], tiles_f[:, :], -float(P), float(REGION), ALU.mult, ALU.add))
                dve.wait_ge(numbered, 1)
                per_tile = lambda v: v.rearrange("p (o e) -> p o e", o=1).to_broadcast([1, TILES, E])
                next_step(dve.tensor_tensor(past[:, :, :], tile_no[:, :].rearrange("p (j o) -> p j o", o=1)
                                            .to_broadcast([1, TILES, E]), per_tile(upto[:, :]), ALU.is_ge))
                next_step(dve.tensor_reduce(expert_f[:, :], past[:, :, :], AX.X, ALU.add))
                next_step(dve.tensor_scalar(expert_of[:, :], expert_f[:, :], float(E - 1), None, ALU.min))
                next_step(dve.tensor_scalar(weights_of[:, :], expert_f[:, :], float(E - 1), float(SPAN),
                                            ALU.min, ALU.mult))
                next_step(dve.tensor_tensor(past[:, :, :], past[:, :, :], per_tile(jump[:, :]), ALU.mult))
                next_step(dve.tensor_reduce(offset_f[:, :], past[:, :, :], AX.X, ALU.add))
                next_step(dve.scalar_tensor_tensor(row_f[:, :], tile_no[:, :], float(P), offset_f[:, :],
                                                   ALU.mult, ALU.add))
                next_step(dve.tensor_scalar(row_c[:, :], row_f[:, :], float(E * REGION), None, ALU.min))
                dve.tensor_copy(row_of[:, :], row_c[:, :]).then_inc(table, 1)

                split(RAWS, len(STAGED))

                def expert(j):
                    return dve.value_load(expert_of[0:1, bass.ds(j, 1)], min_val=0, max_val=E - 1)

                def x_part(j, u):
                    dve.wait_ge(x_hi, j + 1)
                    dve.tensor_tensor(xst[1][:, u % 2, :, :], bank_x[u % 2][:, 0:D].rearrange("p (c t) -> p c t", c=DC),
                                      xst[0][:, u % 2, :, :].bitcast(F32), ALU.subtract).then_inc(x_lo, 1)

                def tags(j, u):
                    due(dve, added, (j + 1 - STEPS) * 16)
                    dve.wait_ge(x_full, j + 1)
                    dve.tensor_copy(tag[:, u % STEPS, 0:1], xs[:, u % STEPS, D:D + 1])
                    dve.tensor_copy(number[:, u % STEPS, :], xs[:, u % STEPS, D + 1:D + 2]).then_inc(tagged, 1)

                def bias1(j, u, e):
                    dve.wait_ge(h_full, j + 1)
                    dve.tensor_tensor(hid[:, u % 2, :], bank_h[u % 2][:, :], b1_all[:, bass.ds(e * H, H)],
                                      ALU.add).then_inc(h_biased, 1)

                def h_part(j, u):
                    dve.wait_ge(ht_hi, j + 1)
                    dve.scalar_tensor_tensor(hidt[1][:, u % 2, :, :],
                                             bank_ht[u % 2][:, :].rearrange("p (c t) -> p c t", c=HC), 0.0,
                                             hidt[0][:, u % 2, :, :].bitcast(F32), ALU.max,
                                             ALU.subtract).then_inc(ht_lo, 1)

                def bias2(j, u, e):
                    dve.wait_ge(y_full, j + 1)
                    due(dve, y_weighted, j - 1)
                    dve.tensor_tensor(ysum[:, u % 2, :], bank_y[u % 2][:, 0:D], b2_all[:, bass.ds(e * D, D)],
                                      ALU.add).then_inc(y_biased, 1)

                dve.wait_ge(bias_in, 32)

                def body(j0, last):
                    if isinstance(j0, int) and j0 == 0:
                        dve.wait_ge(table, 18)
                        x_part(0, 0)
                        x_part(1, 1)
                        bias1(0, 0, expert(0))
                    here = expert(j0)
                    for u in range(STEPS):
                        behind = expert(j0 + u + 1) if not last or u < STEPS - 1 else None
                        h_part(j0 + u, u)
                        if not last or u < STEPS - 2:
                            x_part(j0 + u + 2, u + 2)
                        if behind is not None:
                            bias1(j0 + u + 1, u + 1, behind)
                        tags(j0 + u, u)
                        bias2(j0 + u, u, here)
                        here = behind

                tiles(dve, body)

            @block.tensor
            def _(pe):
                def three(dst, stat, move, start, stop):
                    for m, (s, r) in enumerate(((0, 1), (1, 0), (0, 0))):
                        last = pe.matmul(dst, stat[s], move[r], start=start and m == 0, stop=stop and m == 2)
                    return last

                def expert(j):
                    return pe.value_load(weights_of[0:1, bass.ds(j, 1)], min_val=0, max_val=(E - 1) * SPAN)

                def turn_x(j, u):
                    if isinstance(j, int):
                        pe.wait_ge(x_tile[u % STEPS], 16 * (j // STEPS + 1))
                    else:
                        pe.wait_ge(x_tile[u % STEPS], (j - u % STEPS) * (16 // STEPS) + 16)
                    for c in range(DC):
                        last = pe.transpose(bank_x[u % 2][:, c * P:(c + 1) * P], xs[:, u % STEPS, c * P:(c + 1) * P],
                                            ident[:, :])
                    last.then_inc(x_full, 1)

                def up(j, u, e):
                    pe.wait_ge(x_lo, j + 1)
                    for c in range(DC):
                        last = three(bank_h[u % 2][:, :], [xst[s][:, u % 2, c, :] for s in range(2)],
                                     [w1[s][:, bass.ds(e + c * H, H)] for s in range(2)], c == 0, c == DC - 1)
                    last.then_inc(h_full, 1)

                def turn_h(j, u):
                    pe.wait_ge(h_biased, j + 1)
                    for c in range(HC):
                        last = pe.transpose(bank_ht[u % 2][:, c * P:(c + 1) * P], hid[:, u % 2, c * P:(c + 1) * P],
                                            ident[:, :])
                    last.then_inc(ht_full, 1)

                def down(j, u, e):
                    pe.wait_ge(ht_lo, j + 1)
                    for c in range(HC):
                        last = three(bank_y[u % 2][:, 0:D], [hidt[s][:, u % 2, c, :] for s in range(2)],
                                     [w2[s][:, bass.ds(e + c * D, D)] for s in range(2)], c == 0, c == HC - 1)
                    last.then_inc(y_full, 1)

                def body(j0, last):
                    if isinstance(j0, int) and j0 == 0:
                        turn_x(0, 0)
                        turn_x(1, 1)
                        up(0, 0, expert(0))
                    here = None
                    for u in range(STEPS):
                        turn_h(j0 + u, u)
                        if not last or u < STEPS - 2:
                            turn_x(j0 + u + 2, u + 2)
                        behind = expert(j0 + u + 1) if not last or u < STEPS - 1 else None
                        if behind is not None:
                            up(j0 + u + 1, u + 1, behind)
                        if here is None:
                            here = expert(j0)
                        down(j0 + u, u, here)
                        here = behind

                pe.wait_ge(table, 18)
                pe.wait_ge(stage_lo, len(STAGED))
                tiles(pe, body)


def kernel(x, ctx_768, L0_xattn_w_q, L0_xattn_w_k, L0_xattn_w_v, L0_xattn_w_o, L0_xattn_b_o, L0_ffn_gate,
           L0_ffn_W1, L0_ffn_b1, L0_ffn_W2, L0_ffn_b2):
    import concourse.bacc as bacc
    from concourse.bass_utils import run_bass_kernel_spmd

    nc = bacc.Bacc("TRN2", target_bir_lowering=False, num_devices=1)
    B, S, D = x.shape
    given = {
        "x": np.ascontiguousarray(x).reshape(B * S, D),
        "ctx": np.ascontiguousarray(ctx_768).reshape(B * S, -1),
        "w_q": L0_xattn_w_q, "w_k": L0_xattn_w_k, "w_v": L0_xattn_w_v, "w_o": L0_xattn_w_o, "b_o": L0_xattn_b_o,
        "gate": L0_ffn_gate, "W1": L0_ffn_W1, "b1": L0_ffn_b1, "W2": L0_ffn_W2, "b2": L0_ffn_b2,
    }
    arrays = {f"in_{k}": np.ascontiguousarray(v) for k, v in given.items()}
    aps = [nc.dram_tensor(k, a.shape, mybir.dt.from_np(a.dtype), kind="ExternalInput").ap() for k, a in arrays.items()]
    out = nc.dram_tensor("out", (B * S + P, D), F32, kind="ExternalOutput").ap()
    program(nc, *aps, out)
    r = run_bass_kernel_spmd(nc, [arrays], core_ids=[0])
    return r.results[0]["out"][:B * S].reshape(B, S, D)
```

```python
from contextlib import ExitStack

import numpy as np

import concourse.bass as bass
from concourse import mybir

F32, F32R, I32, BF16 = mybir.dt.float32, mybir.dt.float32r, mybir.dt.int32, mybir.dt.bfloat16
ALU = mybir.AluOpType
ACT = mybir.ActivationFunctionType
AX = mybir.AxisListType

P = 128
HEAD = 64
EPS_LN = 1e-5
GUARD = 1e-12
TOP = 2
BIG = float(1 << 17)
EARLIER, PREV, CUR, NEXT = "earlier", "prev", "cur", "next"


class Signal:

    def __init__(self, sem, events, pairs):
        self.sem, self.events, self.pairs = sem, events, pairs

    def present(self, it):
        last = {EARLIER: self.pairs + 1, PREV: self.pairs, CUR: self.pairs - 1, NEXT: self.pairs - 2}
        first = {EARLIER: 2, PREV: 1, CUR: 0, NEXT: -1}
        return [name for name, of in self.events if first[of] <= it <= last[of]]

    def before(self, it):
        return sum(len(self.present(j)) for j in range(-1, it))

    def at(self, it, name):
        if isinstance(it, int):
            here = self.present(it)
            return self.before(it) + here.index(name) + 1 if name in here else 0
        names = [n for n, _ in self.events]
        return it * len(names) + (self.before(2) - 2 * len(names) + names.index(name) + 1)


def wait(engine, signal, it, name, back=0):
    value = signal.at(it, name)
    if isinstance(value, int):
        value -= back
        if value > 0:
            engine.wait_ge(signal.sem, value)
    else:
        engine.wait_ge(signal.sem, value - back)


def program(nc, x, ctx, w_q, w_k, w_v, w_o, b_o, gate, W1, b1, W2, b2, out):
    tokens, D = x.shape
    C = ctx.shape[1]
    INNER = w_q.shape[1]
    HEADS = INNER // HEAD
    E, _, H = W1.shape
    PAIRS = tokens // (2 * P)
    HALF = HEADS // 2
    CHUNKS = INNER // P
    SCALE = HEAD ** -0.5
    DC = D // P
    HC = H // P
    TILE = 2 * P
    REGION = tokens + TILE
    TILES = TOP * tokens // TILE + E
    ROW = D + 2
    assert C == P + HEAD and D == 2 * P and HEADS == 16 and TILES % 2 == 0 and PAIRS >= 4

    lists = nc.dram_tensor("lists", ((E + 1) * REGION, ROW), F32, kind="Internal").ap()

    A_SLOTS = [
        [("v00", CUR), ("o0", PREV)],
        [("q10", CUR), ("k10", CUR)],
        [("v01", CUR), ("o1", PREV), ("f0", EARLIER), ("f1", EARLIER)],
        [("q11", CUR), ("k11", CUR), ("v10", CUR)],
        [("v11", CUR), ("t0", NEXT), ("t1", NEXT)],
        [("y0", PREV), ("y1", PREV), ("q00", NEXT)],
        [("k00", NEXT), ("q01", NEXT), ("l0", PREV)],
        [("k01", NEXT)],
    ]
    A_EVENTS = [e for slot in A_SLOTS for e in slot]
    A_BANKS = 3
    assert len(A_EVENTS) % A_BANKS == 0
    HI_EVENTS = [e for e in A_EVENTS if e[0][0] in "tqk"]
    UNITS = [(f"u{n}", CUR) for n in range(8)]
    LATE = [("u6", PREV), ("u7", PREV)] + [(f"u{n}", CUR) for n in range(6)]
    NEAR = [("u7", PREV)] + [(f"u{n}", CUR) for n in range(7)]
    LAST = [("u5", PREV), ("u6", PREV), ("u7", PREV)] + [(f"u{n}", CUR) for n in range(5)]

    ex = ExitStack()
    with ex:
        def sem(name):
            return ex.enter_context(nc.semaphore(name))

        def signal(name, events):
            return Signal(sem(name), events, PAIRS)

        psum = [ex.enter_context(nc.psum_tensor(f"bank_{n}", [P, 512], F32))
                for n in ("a0", "a1", "a2", "s0", "s1", "t0", "t1", "v")]
        bank_a, bank_s, bank_t, bank_v = psum[0:3], psum[3:5], psum[5:7], psum[7]

        def sb_in(stack):
            return lambda name, shape, dt=F32: stack.enter_context(nc.sbuf_tensor(name, shape, dt))

        keep = sb_in(ex)
        ident = keep("ident", [P, P])
        before = keep("before", [P, E, E])
        run = keep("run", [P, E])
        region0 = keep("region0", [P, E])
        RAWS = 5
        UNIT = 1024
        STEPS = 4
        SPARE = STEPS * 2 * ROW - 2 * UNIT
        stage = keep("stage", [P, RAWS * UNIT + SPARE])
        pad = keep("pad", [P, 2, ROW])

        STAGED = []
        for e in range(E):
            STAGED.append((W1[e, :, :].rearrange("(c p) h -> p c h", p=P), (0, e), DC))
            STAGED.append((W2[e, :, :].rearrange("(c p) d -> p c d", p=P), (1, e), HC))

        def staged(n, parts):
            return stage[:, n % RAWS * UNIT:(n % RAWS + 1) * UNIT].rearrange("p (a b) -> p a b", a=parts)

        stage_in = [sem(f"stage_in{n}") for n in range(RAWS)]

        const = sem("constants")
        made = sem("made")
        with ExitStack() as a:
            sb = sb_in(a)
            upper = sb("upper", [P, P], BF16)
            all_ones = sb("all_ones", [P, P], BF16)
            ones = sb("ones", [P, 2])
            after = sb("after", [P, E, E])
            eps = sb("eps", [P, 2])
            mhalf = sb("mhalf", [P, 2])
            step_id = sb("step_id", [P, 2])
            token_id = sb("token_id", [P, 2])
            bo = sb("bo", [P, D])
            gate_sb = sb("gate_sb", [P, DC, E])
            wq = [sb(f"wq_{s}", [P, DC, INNER], F32R) for s in "hl"]
            wk = [sb(f"wk_{s}", [P, INNER], F32R) for s in "hl"]
            wv = [sb(f"wv_{s}", [P, INNER], F32R) for s in "hl"]
            wk2 = sb("wk2", [P, INNER], F32R)
            wv2 = sb("wv2", [P, INNER], F32R)
            wo = [sb(f"wo_{s}", [P, CHUNKS, D], F32R) for s in "hl"]

            xin = sb("xin", [P, 2, D])
            cin = sb("cin", [P, 2, 2 * P])
            xres = sb("xres", [P, 2, D])
            xn = sb("xn", [P, 2, D])
            xt = [sb(f"xt_{s}", [P, DC + 2, 2 * P], F32R) for s in "hl"]
            qt = [sb(f"qt_{s}", [P, 2, CHUNKS // 2, 2 * P], F32R) for s in "hl"]
            kt = [sb(f"kt_{s}", [P, 2, 2, CHUNKS // 2, 2, P], F32R) for s in "hl"]
            vv = sb("vv", [P, 2, 2, HALF * HEAD])
            prob = sb("prob", [P, 4, 4, P])
            probt = sb("probt", [P, 2, 4, P])
            ot = [sb(f"ot_{s}", [P, 2, CHUNKS, P], F32R) for s in "hl"]
            x1 = sb("x1", [P, 2, D])
            rows = sb("rows", [P, 2, 2, ROW])
            xn2 = sb("xn2", [P, 2, D])
            yt = sb("yt", [P, 2, DC, P])
            low = sb("low", [P, 4, 4])
            total = sb("total", [P, 4, 4])
            inv = sb("inv", [P, 4, 4])
            stats = sb("stats", [P, 2, 2, 6])
            mean_var = sb("mean_var", [P, 2, 2, 2])
            shifted = sb("shifted", [P, 2, 2])
            rstd = sb("rstd", [P, 2, 2])
            small = lambda name, *s, dt=F32: sb(name, [P, 2, *s], dt)
            g_max, g_sum, g_inv = small("g_max"), small("g_sum"), small("g_inv")
            g_log = small("g_log", E)
            g_dif, g_exp, g_raw = small("g_dif", E), small("g_exp", E), small("g_raw", E)
            g_ge, g_gt = small("g_ge", E, E), small("g_gt", E, E)
            g_gem, g_gtm, g_cmp = small("g_gem", E, E), small("g_gtm", E, E), small("g_cmp", E, E)
            g_rank, g_sel = small("g_rank", E), small("g_sel", E)
            g_mask = small("g_mask", E, dt=BF16)
            g_ssum, g_smax, g_sinv, g_w = small("g_ssum"), small("g_smax"), small("g_sinv"), small("g_w", E)
            p_pos, p_hi, p_lo = small("p_pos", E), small("p_hi", E), small("p_lo", E)
            p_b, p_a = small("p_b"), small("p_a")
            p_ea, p_eb, p_wa, p_wb = small("p_ea", E), small("p_eb", E), small("p_wa", E), small("p_wb", E)
            spare = sb("spare", [P, 2])
            slot = sb("slot", [P, 2, 2], I32)

            def wide(t, n):
                return t.rearrange("p (m o) -> p m o", o=1).to_broadcast([P, t.shape[1], n])

            w_hi, w_lo = sem("w_hi"), sem("w_lo")
            zeroed = sem("zeroed")
            x_in, c_in, r_in, x1_out = sem("x_in"), sem("c_in"), sem("r_in"), sem("x1_out")
            sent = sem("sent")
            a_full, a_done = signal("a_full", A_EVENTS), signal("a_done", A_EVENTS)
            a_hi = signal("a_hi", HI_EVENTS)
            s_full, s_low, s_exp = signal("s_full", UNITS), signal("s_low", UNITS), signal("s_exp", UNITS)
            s_inv, s_norm = signal("s_inv", NEAR), signal("s_norm", UNITS)
            t_full, t_copy = signal("t_full", LATE), signal("t_copy", LATE)
            v_full, v_hi, v_lo = signal("v_full", LATE), signal("v_hi", LATE), signal("v_lo", LAST)
            dve_step = signal("dve_step", [(s, PREV) for s in (
                "bn2_0", "bn2_1", "agg2", "ln2", "g_max", "g_dif")])
            route_step = signal("route_step", [(s, EARLIER) for s in (
                "g_sum", "g_inv", "g_raw", "g_ge", "g_gt", "g_gem", "g_gtm", "g_cmp", "g_rank", "g_mask",
                "g_sel", "g_ssum", "g_smax", "g_sinv", "g_w", "p_hi", "p_lo", "p_b", "p_a", "p_ea", "p_eb",
                "p_wa", "p_wb", "wa", "wb", "slot_a", "slot_b")])
            ln1_step = signal("ln1_step", [("bn1_0", NEXT), ("bn1_1", NEXT), ("agg1", NEXT), ("ln1", NEXT)])
            pool_step = signal("pool_step", [
                ("first", EARLIER), ("twice", EARLIER), ("ids", EARLIER), ("next_id", EARLIER),
                ("shift1", NEXT), ("rstd1", NEXT), ("shift2", PREV), ("rstd2", PREV), ("xres", CUR)])
            routed = signal("routed", [("routed", EARLIER)])
            g_exps = signal("g_exps", [("g_exp", PREV)])

            WEIGHTS = [([w_q[c * P:(c + 1) * P, :]], wq[0][:, c, :], wq[1][:, c, :]) for c in range(DC)]
            for w, d, d2 in ((w_k, wk, wk2), (w_v, wv, wv2)):
                WEIGHTS.append(([w[0:P, :]], d[0][:, :], d[1][:, :]))
                WEIGHTS.append(([w[P:C, :], w[P:C, :]], d2[:, :], None))
            for c in range(0, CHUNKS, 4):
                WEIGHTS.append(([w_o[c * P:(c + 4) * P, :].rearrange("(c p) d -> p c d", p=P)],
                                wo[0][:, c:c + 4, :], wo[1][:, c:c + 4, :]))
            NW = len(WEIGHTS)
            Q_READY, K_READY, V_READY = DC, DC + 2, DC + 4
            WHEN = {(-1, 4): (0, Q_READY), (-1, 5): (Q_READY, K_READY), (-1, 7): (K_READY, V_READY),
                    (0, 4): (V_READY, NW)}

            assert INNER == 4 * D == 1024
            w_raw = [sem(f"w_raw{n}") for n in range(NW)]
            stage_more = sb("stage_more", [P, NW - RAWS, 1024])

            def raw_of(n, like=None):
                raw = stage[:, n * UNIT:(n + 1) * UNIT] if n < RAWS else stage_more[:, n - RAWS, :]
                return raw.rearrange("p (c d) -> p c d", c=4) if like is not None and len(like.shape) == 3 else raw

            def iterations(engine, body):
                body(-1)
                body(0)
                body(1)
                with engine.Fori(2, PAIRS - 1) as it:
                    body(it)
                body(PAIRS - 1)
                body(PAIRS)
                body(PAIRS + 1)

            def has(it, of):
                first, last = {EARLIER: (2, PAIRS + 1), PREV: (1, PAIRS), CUR: (0, PAIRS - 1), NEXT: (-1, PAIRS - 2)}[of]
                return not isinstance(it, int) or first <= it <= last

            def a_bank(it, name):
                here = a_full.present(it) if isinstance(it, int) else [n for n, _ in A_EVENTS]
                return bank_a[(a_full.before(it if isinstance(it, int) else 2) + here.index(name)) % A_BANKS]

            block = a.enter_context(nc.Block())

            @block.sync
            def _(sp):
                def load_x(it):
                    row = (it + 1) * (2 * P)
                    src = x[bass.ds(row, 2 * P), :].rearrange("(b p) d -> p b d", p=P)
                    sp.dma_start(xin[:, :, :], src).then_inc(x_in, 16)
                    cs = ctx[bass.ds(row, 2 * P), :].rearrange("(b p) d -> p b d", p=P)
                    sp.dma_start(cin[:, :, 0:C], cs).then_inc(c_in, 16)
                    sp.dma_start(cin[:, :, C:2 * P], cs[:, :, P:C]).then_inc(c_in, 16)

                load_x(-1)
                for n, (sources, hi, _) in enumerate(WEIGHTS):
                    rows_each = P // len(sources)
                    for k, src in enumerate(sources):
                        sp.dma_start(raw_of(n, hi)[k * rows_each:(k + 1) * rows_each], src).then_inc(w_raw[n], 16)
                sp.dma_start(bo[:, :], b_o.rearrange("(o d) -> o d", o=1).to_broadcast([P, D])).then_inc(const, 16)
                sp.dma_start(gate_sb[:, :, :], gate.rearrange("(c p) e -> p c e", p=P)).then_inc(const, 16)
                sp.wait_ge(made, 19)
                sp.dma_start(out[tokens:tokens + TILE, :].rearrange("(b p) d -> p b d", p=P),
                             pad[:, :, 0:D]).then_inc(x1_out, 16)

                def body(it):
                    if has(it, NEXT) and not (isinstance(it, int) and it < 0):
                        wait(sp, ln1_step, it - 1, "ln1")
                        wait(sp, a_full, it - 1, "q00")
                        load_x(it)
                    if has(it, PREV):
                        wait(sp, a_done, it, "o1")
                        dst = out[bass.ds((it - 1) * (2 * P), 2 * P), :].rearrange("(b p) d -> p b d", p=P)
                        sp.dma_start(dst, x1[:, :, :]).then_inc(x1_out, 16)
                    if has(it, CUR):
                        src = x[bass.ds(it * (2 * P), 2 * P), :].rearrange("(b p) d -> p b d", p=P)
                        sp.dma_start(xres[:, :, :], src).then_inc(r_in, 16)

                body(-1)
                body(0)
                for n, (src, dst, parts) in enumerate(STAGED[:RAWS]):
                    sp.wait_ge(w_lo, n + 1)
                    sp.dma_start(staged(n, parts), src).then_inc(stage_in[n], 16)
                body(1)
                with sp.Fori(2, PAIRS - 1) as it:
                    body(it)
                body(PAIRS - 1)
                body(PAIRS)
                body(PAIRS + 1)
                sp.wait_ge(x1_out, 16 * (PAIRS + 1))

            @block.gpsimd
            def _(pool):
                pool.memset(ident[:, :], 0.0).then_inc(made, 1)
                pool.memset(upper[:, :], 0.0).then_inc(made, 1)
                pool.memset(ones[:, :], 1.0).then_inc(made, 1)
                pool.memset(all_ones[:, :], 1.0).then_inc(made, 1)
                pool.memset(before[:, :, :], 0.0).then_inc(made, 1)
                pool.memset(after[:, :, :], 0.0).then_inc(made, 1)
                pool.memset(eps[:, :], EPS_LN).then_inc(made, 1)
                pool.memset(mhalf[:, :], -0.5).then_inc(made, 1)
                pool.memset(step_id[:, :], 2.0 * P).then_inc(made, 1)
                pool.memset(spare[:, :], 0.0).then_inc(made, 1)
                pool.memset(pad[:, :, 0:ROW - 1], 0.0).then_inc(made, 1)
                pool.iota(token_id[:, :], [[P, 2]], base=0, channel_multiplier=1,
                          allow_small_or_imprecise_dtypes=True).then_inc(made, 1)
                pool.iota(pad[:, :, ROW - 1], [[P, 2]], base=tokens, channel_multiplier=1,
                          allow_small_or_imprecise_dtypes=True).then_inc(made, 1)
                pool.iota(run[:, :], [[REGION, E]], base=0, channel_multiplier=0,
                          allow_small_or_imprecise_dtypes=True).then_inc(made, 1)
                pool.iota(region0[:, :], [[REGION, E]], base=0, channel_multiplier=0,
                          allow_small_or_imprecise_dtypes=True).then_inc(made, 1)
                pool.wait_ge(made, 15)
                pool.affine_select(out=ident[:, :], in_=ident[:, :], compare_op=ALU.not_equal, fill=1.0,
                                   base=0, pattern=[[-1, P]], channel_multiplier=1).then_inc(made, 1)
                pool.affine_select(out=upper[:, :], in_=upper[:, :], compare_op=ALU.is_ge, fill=1.0,
                                   base=0, pattern=[[-1, P]], channel_multiplier=1).then_inc(made, 1)
                pool.affine_select(out=before[:, :, :], in_=before[:, :, :], compare_op=ALU.is_ge, fill=1.0,
                                   base=0, pattern=[[-1, E], [1, E]], channel_multiplier=0).then_inc(made, 1)
                pool.affine_select(out=after[:, :, :], in_=after[:, :, :], compare_op=ALU.is_ge, fill=1.0,
                                   base=0, pattern=[[1, E], [-1, E]], channel_multiplier=0).then_inc(made, 1)
                pool.wait_ge(made, 19)

                def rstd_of(it, k):
                    if k == 0:
                        wait(pool, ln1_step, it, "agg1")
                    else:
                        wait(pool, dve_step, it, "agg2")
                    pool.tensor_tensor(shifted[:, k, :], mean_var[:, k, :, 1], eps[:, :],
                                       ALU.add).then_inc(pool_step.sem, 1)
                    wait(pool, pool_step, it, f"shift{k + 1}")
                    pool.tensor_tensor(rstd[:, k, :], shifted[:, k, :], mhalf[:, :],
                                       ALU.pow).then_inc(pool_step.sem, 1)

                def norm(it, n):
                    wait(pool, s_inv, it + 1 if n == 7 else it, f"u{n}")
                    pool.tensor_tensor(prob[:, n % 4, :, :], prob[:, n % 4, :, :], wide(inv[:, n % 4, :], P),
                                       ALU.mult).then_inc(s_norm.sem, 1)

                def body(it):
                    for n in range(8):
                        if n == 2 and has(it, NEXT):
                            rstd_of(it, 0)
                            if isinstance(it, int) and it == -1:
                                zero_keys()
                                pool.wait_ge(const, 32)
                        if n == 3 and has(it, PREV):
                            rstd_of(it, 1)
                        if n == 1 and has(it, EARLIER):
                            wait(pool, dve_step, it - 1, "ln2")
                            pool.wait_ge(sent, (it - 2) * 64 + 16)
                            for k in range(2):
                                pool.tensor_tensor(rows[:, :, k, 0:D], xn2[:, :, :], wide(ones[:, :], D),
                                                   ALU.mult).then_inc(pool_step.sem, 1)
                            pool.tensor_tensor(rows[:, :, :, D + 1], wide(token_id[:, :], 2), wide(ones[:, :], 2),
                                               ALU.mult).then_inc(pool_step.sem, 1)
                            wait(pool, pool_step, it, "ids")
                            pool.tensor_tensor(token_id[:, :], token_id[:, :], step_id[:, :],
                                               ALU.add).then_inc(pool_step.sem, 1)
                        if has(it, CUR):
                            norm(it, n)
                        if n == 6 and has(it, EARLIER):
                            wait(pool, route_step, it, "slot_b")
                            wait(pool, pool_step, it, "next_id")
                            pool.tensor_tensor(spare[:, 1:2], spare[:, 0:1], spare[:, 0:1],
                                               ALU.mult).then_inc(routed.sem, 1)
                        if n in (6, 7) and has(it, EARLIER):
                            for k in range(2):
                                pool.indirect_dma_start(
                                    lists, bass.IndirectOffsetOnAxis(ap=slot[:, k, n - 6:n - 5], axis=0),
                                    rows[:, n - 6, k, :], None).then_inc(sent, 16)
                    if has(it, CUR):
                        pool.wait_ge(r_in, (it + 1) * 16)
                        pool.tensor_tensor(xres[:, :, :], xres[:, :, :],
                                           bo[:, :].rearrange("p (o d) -> p o d", o=1).to_broadcast([P, 2, D]),
                                           ALU.add).then_inc(pool_step.sem, 1)

                def zero_keys():
                    wait(pool, pool_step, -1, "rstd1")
                    for side in range(2):
                        part = slice((1 - side) * HEAD, (2 - side) * HEAD)
                        for s in range(2):
                            pool.memset(kt[s][part, :, :, :, side, :].bitcast(F32), 0.0).then_inc(zeroed, 1)
                        pool.wait_ge(zeroed, 2 * (side + 1))

                pool.dma_start(lists[E * REGION:E * REGION + TILE, :].rearrange("(b p) d -> p b d", p=P),
                               pad[:, :, :]).then_inc(sent, 16)
                iterations(pool, body)
                pool.wait_ge(sent, 64 * PAIRS + 16)

            @block.scalar
            def _(act):
                def prepare(first, last):
                    for n in range(first, last):
                        sources, hi, _ = WEIGHTS[n]
                        act.wait_ge(w_raw[n], 16 * len(sources))
                        act.activation(hi, raw_of(n, hi), ACT.Copy).then_inc(w_hi, 1)

                def copy_t(it, name, n):
                    wait(act, t_full, it, name)
                    act.activation(probt[:, n % 2, :, :], bank_t[n % 2][:, :].rearrange("p (h q) -> p h q", h=4),
                                   ACT.Copy).then_inc(t_copy.sem, 1)

                def exps(it, n):
                    wait(act, s_low, it, f"u{n}")
                    for h in range(4):
                        e = act.activation(prob[:, n % 4, h, :], bank_s[n % 2][:, h * P:(h + 1) * P], ACT.Exp,
                                           bias=low[:, n % 4, h:h + 1], scale=-1.0,
                                           accum_out=total[:, n % 4, h:h + 1])
                    e.then_inc(s_exp.sem, 1)

                def hi_part(it, name):
                    wait(act, a_full, it, name)
                    src = a_bank(it, name)
                    kind, k = name[0], int(name[-1])
                    if kind == "t":
                        last = act.activation(xt[0][:, :, k * P:(k + 1) * P],
                                              src[:, :].rearrange("p (c t) -> p c t", c=DC + 2), ACT.Copy)
                    elif kind == "q":
                        last = act.activation(qt[0][:, int(name[1]), 2 * k:2 * k + 2, :],
                                              src[:, :].rearrange("p (c t) -> p c t", c=2), ACT.Copy, scale=-SCALE)
                    else:
                        for side in range(2):
                            part = slice(side * HEAD, (side + 1) * HEAD)
                            last = act.activation(
                                kt[0][part, int(name[1]), :, 2 * k:2 * k + 2, side, :],
                                src[part, :].rearrange("p (c b t) -> p b c t", c=2, b=2), ACT.Copy)
                    last.then_inc(a_hi.sem, 1)

                def hi_out(it, name, n):
                    wait(act, v_full, it, name)
                    c = 4 * (n // 4) + 2 * (n % 2)
                    act.activation(ot[0][:, (n % 4) // 2, c:c + 2, :],
                                   bank_v[:, 0:2 * P].rearrange("p (c q) -> p c q", c=2), ACT.Copy).then_inc(v_hi.sem, 1)

                def body(it):
                    for n in range(8):
                        if isinstance(it, int) and (it, n) in WHEN:
                            prepare(*WHEN[it, n])
                        late, of = LATE[n]
                        if has(it, of):
                            copy_t(it, late, (n - 2) % 8)
                        if has(it, CUR):
                            exps(it, n)
                        for name, o in A_SLOTS[n]:
                            if (name, o) in HI_EVENTS and has(it, o):
                                hi_part(it, name)
                        if has(it, of):
                            hi_out(it, late, (n - 2) % 8)
                        if n == 7 and has(it, PREV):
                            wait(act, dve_step, it, "g_dif")
                            act.activation(g_exp[:, :, :], g_dif[:, :, :], ACT.Exp).then_inc(g_exps.sem, 1)

                iterations(act, body)

            @block.vector
            def _(dve):
                def prepare(first, last):
                    for n in range(first, last):
                        dve.wait_ge(w_hi, n + 1)
                        _, hi, lo = WEIGHTS[n]
                        raw = raw_of(n, hi)
                        if lo is None:
                            raw, hi = raw[HEAD:P], hi[HEAD:P]
                            lo = hi
                        dve.tensor_tensor(lo, raw, hi.bitcast(F32), ALU.subtract).then_inc(w_lo, 1)

                done, routes = dve_step.sem, route_step.sem
                steps = (ln1_step.sem, dve_step.sem)

                def after_step(it, name):
                    wait(dve, dve_step, it, name)

                def lowest(it, n):
                    wait(dve, s_full, it, f"u{n}")
                    dve.tensor_reduce(low[:, n % 4, :], bank_s[n % 2][:, :].rearrange("p (h k) -> p h k", h=4),
                                      AX.X, ALU.min).then_inc(s_low.sem, 1)

                def inverse(it, name, n):
                    wait(dve, s_exp, it - 1 if n == 7 else it, name)
                    dve.reciprocal(inv[:, n % 4, :], total[:, n % 4, :]).then_inc(s_inv.sem, 1)

                def second_part(it, name):
                    src = a_bank(it, name)
                    kind, k = name[0], int(name[-1])
                    if (kind in "tqk"):
                        wait(dve, a_hi, it, name)
                    else:
                        wait(dve, a_full, it, name)
                    if kind == "t":
                        last = dve.tensor_tensor(xt[1][:, :, k * P:(k + 1) * P],
                                                 src[:, :].rearrange("p (c t) -> p c t", c=DC + 2),
                                                 xt[0][:, :, k * P:(k + 1) * P].bitcast(F32), ALU.subtract)
                    elif kind == "q":
                        g = int(name[1])
                        last = dve.scalar_tensor_tensor(qt[1][:, g, 2 * k:2 * k + 2, :],
                                                        src[:, :].rearrange("p (c t) -> p c t", c=2), -SCALE,
                                                        qt[0][:, g, 2 * k:2 * k + 2, :].bitcast(F32),
                                                        ALU.mult, ALU.subtract)
                    elif kind == "k":
                        for side in range(2):
                            part = slice(side * HEAD, (side + 1) * HEAD)
                            at = (part, int(name[1]), slice(None), slice(2 * k, 2 * k + 2), side, slice(None))
                            last = dve.tensor_tensor(kt[1][at], src[part, :].rearrange("p (c b t) -> p b c t", c=2, b=2),
                                                     kt[0][at].bitcast(F32), ALU.subtract)
                    elif kind == "v":
                        last = dve.tensor_copy(vv[:, int(name[1]), k, :], src[:, :])
                    elif kind == "o":
                        wait(dve, pool_step, it - 1, "xres")
                        if k == 0:
                            dve.wait_ge(x1_out, it * 16)
                        last = dve.tensor_tensor(x1[:, k, :], src[:, 0:D], xres[:, k, :], ALU.add)
                    elif kind == "y":
                        last = dve.tensor_copy(yt[:, k, :, :], src[:, 0:D].rearrange("p (c t) -> p c t", c=DC))
                    elif kind == "l":
                        last = dve.tensor_copy(g_log[:, :, :], src[:, 0:2 * E].rearrange("p (b e) -> p b e", b=2))
                    elif k == 0:
                        base = run[:, :].rearrange("p (o e) -> p o e", o=1).to_broadcast([P, 2, E])
                        last = dve.tensor_tensor(p_pos[:, :, :], src[:, 0:2 * E].rearrange("p (b e) -> p b e", b=2),
                                                 base, ALU.add)
                    else:
                        wait(dve, a_done, it, "f0")
                        last = dve.tensor_tensor(run[:, :], src[:, 0:E], run[:, :], ALU.add)
                    last.then_inc(a_done.sem, 1)

                def low_out(it, name, n):
                    wait(dve, v_hi, it - 1 if n == 5 else it, name)
                    c = 4 * (n // 4) + 2 * (n % 2)
                    dve.tensor_tensor(ot[1][:, (n % 4) // 2, c:c + 2, :],
                                      bank_v[:, 0:2 * P].rearrange("p (c q) -> p c q", c=2),
                                      ot[0][:, (n % 4) // 2, c:c + 2, :].bitcast(F32),
                                      ALU.subtract).then_inc(v_lo.sem, 1)

                def statistics(k, src):
                    for b in range(2):
                        dve.bn_stats(stats[:, k, b, :], src[:, b, :]).then_inc(steps[k], 1)

                def aggregate(k):
                    for b in range(2):
                        last = dve.bn_aggr(mean_var[:, k, b, :], stats[:, k, b, :])
                    last.then_inc(steps[k], 1)

                def normalise(it, k, src, dst):
                    wait(dve, pool_step, it, f"rstd{k + 1}")
                    for b in range(2):
                        last = dve.tensor_scalar(dst[b], src[:, b, :], mean_var[:, k, b, 0:1], rstd[:, k, b:b + 1],
                                                 ALU.subtract, ALU.mult)
                    last.then_inc(steps[k], 1)

                def gate_scores(it):
                    wait(dve, a_done, it, "l0")
                    dve.tensor_reduce(g_max[:, :], g_log[:, :, :], AX.X, ALU.max).then_inc(done, 1)
                    after_step(it, "g_max")
                    dve.tensor_tensor(g_dif[:, :, :], g_log[:, :, :], wide(g_max[:, :], E), ALU.subtract).then_inc(done, 1)

                def gate_top(it):
                    wait(dve, g_exps, it - 1, "g_exp")
                    dve.tensor_reduce(g_sum[:, :], g_exp[:, :, :], AX.X, ALU.add).then_inc(routes, 1)
                    wait(dve, route_step, it, "g_sum")
                    dve.reciprocal(g_inv[:, :], g_sum[:, :]).then_inc(routes, 1)
                    wait(dve, route_step, it, "g_inv")
                    dve.tensor_tensor(g_raw[:, :, :], g_exp[:, :, :], wide(g_inv[:, :], E), ALU.mult).then_inc(routes, 1)
                    wait(dve, route_step, it, "g_raw")
                    for b in range(2):
                        other = g_raw[:, b, :].rearrange("p (o f) -> p o f", o=1).to_broadcast([P, E, E])
                        last = dve.tensor_tensor(g_ge[:, b, :, :], other, wide(g_raw[:, b, :], E), ALU.is_ge)
                    last.then_inc(routes, 1)
                    for b in range(2):
                        other = g_raw[:, b, :].rearrange("p (o f) -> p o f", o=1).to_broadcast([P, E, E])
                        last = dve.tensor_tensor(g_gt[:, b, :, :], other, wide(g_raw[:, b, :], E), ALU.is_gt)
                    last.then_inc(routes, 1)
                    flat = lambda t: t.rearrange("p b e f -> p b (e f)")
                    both = lambda t: t[:, :, :].rearrange("p e f -> p (e f)").rearrange(
                        "p (o m) -> p o m", o=1).to_broadcast([P, 2, E * E])
                    wait(dve, route_step, it, "g_ge")
                    dve.tensor_tensor(flat(g_gem[:, :, :, :]), flat(g_ge[:, :, :, :]), both(before), ALU.mult).then_inc(routes, 1)
                    wait(dve, route_step, it, "g_gt")
                    dve.tensor_tensor(flat(g_gtm[:, :, :, :]), flat(g_gt[:, :, :, :]), both(after), ALU.mult).then_inc(routes, 1)
                    wait(dve, route_step, it, "g_gtm")
                    dve.tensor_tensor(flat(g_cmp[:, :, :, :]), flat(g_gem[:, :, :, :]), flat(g_gtm[:, :, :, :]),
                                      ALU.add).then_inc(routes, 1)
                    wait(dve, route_step, it, "g_cmp")
                    dve.tensor_reduce(g_rank[:, :, :], g_cmp[:, :, :, :], AX.X, ALU.add).then_inc(routes, 1)
                    wait(dve, route_step, it, "g_rank")
                    dve.tensor_scalar(g_mask[:, :, :], g_rank[:, :, :], float(TOP), None, ALU.is_lt).then_inc(routes, 1)

                def gate_weights(it):
                    wait(dve, route_step, it, "g_mask")
                    dve.tensor_tensor(g_sel[:, :, :], g_mask[:, :, :], g_raw[:, :, :], ALU.mult).then_inc(routes, 1)
                    wait(dve, route_step, it, "g_sel")
                    dve.tensor_reduce(g_ssum[:, :], g_sel[:, :, :], AX.X, ALU.add).then_inc(routes, 1)
                    wait(dve, route_step, it, "g_ssum")
                    dve.tensor_scalar(g_smax[:, :], g_ssum[:, :], GUARD, None, ALU.max).then_inc(routes, 1)
                    wait(dve, route_step, it, "g_smax")
                    dve.reciprocal(g_sinv[:, :], g_smax[:, :]).then_inc(routes, 1)
                    wait(dve, route_step, it, "g_sinv")
                    dve.tensor_tensor(g_w[:, :, :], g_sel[:, :, :], wide(g_sinv[:, :], E), ALU.mult).then_inc(routes, 1)

                def slots_of(it):
                    wait(dve, a_done, it, "f0")
                    dve.tensor_tensor(p_hi[:, :, :], p_pos[:, :, :], g_mask[:, :, :], ALU.mult).then_inc(routes, 1)
                    dve.scalar_tensor_tensor(p_lo[:, :, :], p_pos[:, :, :], -BIG, g_mask[:, :, :],
                                             ALU.add, ALU.mult).then_inc(routes, 1)
                    wait(dve, route_step, it, "p_hi")
                    dve.tensor_reduce(p_b[:, :], p_hi[:, :, :], AX.X, ALU.max).then_inc(routes, 1)
                    wait(dve, route_step, it, "p_lo")
                    dve.tensor_reduce(p_a[:, :], p_lo[:, :, :], AX.X, ALU.min).then_inc(routes, 1)
                    wait(dve, route_step, it, "p_a")
                    dve.tensor_tensor(p_ea[:, :, :], p_lo[:, :, :], wide(p_a[:, :], E), ALU.is_equal).then_inc(routes, 1)
                    dve.tensor_tensor(p_eb[:, :, :], p_hi[:, :, :], wide(p_b[:, :], E), ALU.is_equal).then_inc(routes, 1)
                    wait(dve, route_step, it, "p_eb")
                    dve.tensor_tensor(p_wa[:, :, :], p_ea[:, :, :], g_w[:, :, :], ALU.mult).then_inc(routes, 1)
                    dve.tensor_tensor(p_wb[:, :, :], p_eb[:, :, :], g_w[:, :, :], ALU.mult).then_inc(routes, 1)
                    wait(dve, route_step, it, "p_wb")
                    wait(dve, pool_step, it, "ids")
                    dve.tensor_reduce(rows[:, :, 0, D:D + 1], p_wa[:, :, :], AX.X, ALU.add).then_inc(routes, 1)
                    dve.tensor_reduce(rows[:, :, 1, D:D + 1], p_wb[:, :, :], AX.X, ALU.add).then_inc(routes, 1)
                    dve.tensor_scalar(slot[:, 0, :], p_a[:, :], BIG, None, ALU.add).then_inc(routes, 1)
                    dve.tensor_copy(slot[:, 1, :], p_b[:, :]).then_inc(routes, 1)

                def body(it):
                    for n in range(8):
                        if isinstance(it, int) and (it, n) in WHEN:
                            prepare(*WHEN[it, n])
                        name, of = LAST[n]
                        if has(it, of) and n in (0, 2):
                            low_out(it, name, (n - 3) % 8)
                        if has(it, CUR):
                            lowest(it, n)
                        name, of = LAST[n]
                        if has(it, of) and n not in (0, 2):
                            low_out(it, name, (n - 3) % 8)
                        if n == 2 and has(it, NEXT):
                            wait(dve, ln1_step, it, "bn1_1")
                        if n == 3 and has(it, PREV):
                            after_step(it, "bn2_1")
                        name, of = NEAR[n]
                        if has(it, of):
                            inverse(it, name, (n - 1) % 8)
                        if n == 2 and has(it, NEXT):
                            aggregate(0)
                        if n == 3 and has(it, PREV):
                            aggregate(1)
                        if n == 1 and has(it, PREV):
                            second_part(it, "o0")
                        if n == 1 and has(it, EARLIER):
                            gate_weights(it)
                        if n == 7 and has(it, PREV):
                            second_part(it, "l0")
                            gate_scores(it)
                        if n == 1 and has(it, NEXT):
                            dve.wait_ge(x_in, (it + 2) * 16)
                            statistics(0, xin)
                        if n == 3 and has(it, NEXT):
                            normalise(it, 0, xin, [xn[:, 0, :], xn[:, 1, :]])
                        if n == 4 and has(it, PREV):
                            wait(dve, pool_step, it, "twice")
                            normalise(it, 1, x1, [xn2[:, 0, :], xn2[:, 1, :]])
                        for name, of in A_SLOTS[n]:
                            if has(it, of) and name not in ("o0", "l0"):
                                second_part(it, name)
                        if n == 2 and has(it, PREV):
                            wait(dve, a_done, it, "o1")
                            statistics(1, x1)
                        if n == 5 and has(it, EARLIER):
                            slots_of(it)
                        if n == 0 and has(it, EARLIER):
                            gate_top(it)

                iterations(dve, body)

            @block.tensor
            def _(pe):
                def three(dst, stat, move, start, stop):
                    for m, (s, r) in enumerate(((0, 1), (1, 0), (0, 0))):
                        last = pe.matmul(dst, stat[s], move[r], start=start and m == 0, stop=stop and m == 2)
                    return last

                def transposes(it, name, n):
                    wait(pe, s_norm, it - 1 if n >= 6 else it, name)
                    wait(pe, t_copy, it, name, 2)
                    for h in range(4):
                        last = pe.transpose(bank_t[n % 2][:, h * P:(h + 1) * P], prob[:, n % 4, h, :], ident[:, :])
                    last.then_inc(t_full.sem, 1)

                def scores(it, n):
                    g, b = n // 4, (n % 4) // 2
                    if n % 4 < 2:
                        wait(pe, a_done, it if g else it - 1, f"k{g}{n % 4}")
                    wait(pe, s_exp, it, f"u{n}", 2)
                    for k in range(2):
                        c = 2 * (n % 2) + k
                        last = three(bank_s[n % 2][:, k * 2 * P:(k + 1) * 2 * P],
                                     [qt[s][:, g, c, b * P:(b + 1) * P] for s in range(2)],
                                     [kt[s][:, g, b, c, :, :].rearrange("p s k -> p (s k)") for s in range(2)], True, True)
                    last.then_inc(s_full.sem, 1)

                def values(it, name, n):
                    g, b = n // 4, (n % 4) // 2
                    if g == 0:
                        wait(pe, a_done, it, f"v0{b}")
                    elif n < 6:
                        wait(pe, a_done, it, "v10")
                    else:
                        wait(pe, a_done, it - 1, "v11")
                    wait(pe, t_copy, it, name)
                    before_it = LAST[(n + 2) % 8][0]
                    wait(pe, v_lo, it, before_it)
                    for h in range(4):
                        head = 4 * (n % 2) + h
                        side = slice((h % 2) * HEAD, (h % 2 + 1) * HEAD)
                        last = pe.matmul(bank_v[side, (h // 2) * P:(h // 2 + 1) * P],
                                         vv[:, g, b, head * HEAD:(head + 1) * HEAD], probt[:, n % 2, h, :],
                                         start=True, stop=True, skip_group_check=True)
                    last.then_inc(v_full.sem, 1)

                def product(it, name):
                    dst = a_bank(it, name)
                    kind, k = name[0], int(name[-1])
                    wait(pe, a_done, it, name, A_BANKS)
                    if kind == "t":
                        wait(pe, ln1_step, it, "ln1")
                        pe.wait_ge(c_in, (it + 2) * 32)
                        for c in range(DC):
                            pe.transpose(dst[:, c * P:(c + 1) * P], xn[:, k, c * P:(c + 1) * P], ident[:, :])
                        for c in range(2):
                            last = pe.transpose(dst[:, (DC + c) * P:(DC + c + 1) * P],
                                                cin[:, k, c * P:(c + 1) * P], ident[:, :])
                    elif kind == "q":
                        g = int(name[1])
                        if k == 0:
                            wait(pe, a_done, it if g == 0 else it - 1, "t1" if g == 0 else "q00")
                        for j in range(2):
                            col = slice((4 * g + 2 * k + j) * P, (4 * g + 2 * k + j + 1) * P)
                            for c in range(DC):
                                last = three(dst[:, j * 2 * P:(j + 1) * 2 * P], [wq[s][:, c, col] for s in range(2)],
                                             [xt[s][:, c, :] for s in range(2)], c == 0, c == DC - 1)
                    elif kind == "k":
                        g = int(name[1])
                        for j in range(2):
                            col = slice((4 * g + 2 * k + j) * P, (4 * g + 2 * k + j + 1) * P)
                            o = dst[:, j * 2 * P:(j + 1) * 2 * P]
                            pe.matmul(o, wk2[0:HEAD, col], xt[1][0:HEAD, DC + 1, :], start=True, stop=False)
                            pe.matmul(o, wk2[:, col], xt[0][:, DC + 1, :], start=False, stop=False)
                            last = three(o, [wk[s][:, col] for s in range(2)],
                                         [xt[s][:, DC, :] for s in range(2)], False, True)
                    elif kind == "v":
                        g = int(name[1])
                        col = slice(g * HALF * HEAD, (g + 1) * HALF * HEAD)
                        tok = slice(k * P, (k + 1) * P)
                        pe.matmul(dst[:, :], xt[1][0:HEAD, DC + 1, tok], wv2[0:HEAD, col], start=True, stop=False)
                        pe.matmul(dst[:, :], xt[0][:, DC + 1, tok], wv2[:, col], start=False, stop=False)
                        last = three(dst[:, :], [xt[s][:, DC, tok] for s in range(2)],
                                     [wv[s][:, col] for s in range(2)], False, True)
                    elif kind == "o":
                        wait(pe, v_lo, it, "u5" if k == 0 else "u7")
                        for c in range(CHUNKS):
                            last = three(dst[:, 0:D], [ot[s][:, k, c, :] for s in range(2)],
                                         [wo[s][:, c, :] for s in range(2)], c == 0, c == CHUNKS - 1)
                    elif kind == "y":
                        wait(pe, dve_step, it, "ln2")
                        for c in range(DC):
                            last = pe.transpose(dst[:, c * P:(c + 1) * P], xn2[:, k, c * P:(c + 1) * P], ident[:, :])
                    elif kind == "l":
                        wait(pe, a_done, it, "y1")
                        for b in range(2):
                            for c in range(DC):
                                last = pe.matmul(dst[:, b * E:(b + 1) * E], yt[:, b, c, :], gate_sb[:, c, :],
                                                 start=c == 0, stop=c == DC - 1)
                    elif k == 0:
                        wait(pe, route_step, it, "g_mask")
                        pe.matmul(dst[:, 0:2 * E], upper[:, :], g_mask[:, :, :].rearrange("p b e -> p (b e)"),
                                  start=True, stop=False, skip_group_check=True)
                        last = pe.matmul(dst[:, E:2 * E], all_ones[:, :], g_mask[:, 0, :], start=False, stop=True,
                                         skip_group_check=True)
                    else:
                        for b in range(2):
                            last = pe.matmul(dst[:, 0:E], all_ones[:, :], g_mask[:, b, :], start=b == 0, stop=b == 1)
                    last.then_inc(a_full.sem, 1)

                def body(it):
                    for n in range(8):
                        if isinstance(it, int) and it == -1 and n == 5:
                            pe.wait_ge(w_lo, Q_READY)
                        if isinstance(it, int) and it == -1 and n == 6:
                            pe.wait_ge(w_lo, K_READY)
                        if isinstance(it, int) and it == 0 and n == 0:
                            pe.wait_ge(w_lo, V_READY)
                            pe.wait_ge(zeroed, 4)
                        if isinstance(it, int) and it == 1 and n == 0:
                            pe.wait_ge(w_lo, NW)
                            pe.wait_ge(const, 32)
                        late, of = LATE[n]
                        if has(it, of):
                            transposes(it, late, (n - 2) % 8)
                        if has(it, CUR):
                            scores(it, n)
                        for name, o in A_SLOTS[n]:
                            if has(it, o):
                                product(it, name)
                        if has(it, of):
                            values(it, late, (n - 2) % 8)

                pe.wait_ge(made, 19)
                iterations(pe, body)

        with ExitStack() as stack:
            sb = sb_in(stack)
            SPAN = DC * H
            assert TILES % STEPS == 0 and SPAN == HC * D == 1024 and RAWS == 5 and E * HC <= P
            w1 = [sb(f"w1_{s}", [P, E * SPAN], F32R) for s in "hl"]
            w2 = [sb(f"w2_{s}", [P, E * SPAN], F32R) for s in "hl"]
            b1_rows = sb("b1_rows", [E * HC, P])
            b1t = sb("b1t", [P, E * HC])
            b2_all = sb("b2_all", [P, E * D])
            one = lambda name, *shape, dt=F32: sb(name, [1, *shape], dt)
            count = one("count", E)
            up_i, tiles_i = one("up_i", E, dt=I32), one("tiles_i", E, dt=I32)
            tiles_f, ahead, upto, jump = one("tiles_f", E), one("ahead", E), one("upto", E), one("jump", E)
            ahead_m = one("ahead_m", E, E)
            tile_no = one("tile_no", TILES)
            past = one("past", TILES, E)
            expert_f, offset_f, row_f, row_c = (one("expert_f", TILES), one("offset_f", TILES),
                                                one("row_f", TILES), one("row_c", TILES))
            expert_of = one("expert_of", TILES, dt=I32)
            weights_of = one("weights_of", TILES, dt=I32)
            row_of = one("row_of", TILES, dt=I32)
            end_of = one("end_of", E, dt=I32)
            def in_stage(first, *shape):
                view = stage[:, first:first + int(np.prod(shape))]
                names = "abc"[:len(shape)]
                return view.rearrange(f"p ({' '.join(names)}) -> p {' '.join(names)}", **dict(zip(names, shape)))

            hid = in_stage(0, HC, TILE)
            xs = in_stage(UNIT, STEPS, 2, ROW)
            ysum = in_stage(UNIT + STEPS * 2 * ROW, 2, 2, D)
            yout = in_stage(UNIT + STEPS * 2 * ROW + 4 * D, 2, 2, D)
            tag = sb("tag", [P, STEPS, 2])
            number = sb("number", [P, STEPS, 2], I32)
            xst = [sb(f"xst_{s}", [P, 2, DC, TILE], F32R) for s in "hl"]
            hidt = [sb(f"hidt_{s}", [P, 2, HC, TILE], F32R) for s in "hl"]
            wst = [[sb(f"wst_{h}{k}", [P, SPAN], F32R)[:, :] for k in range(2)] for h in "hl"]
            bst = sb("bst", [P, 2, HC])

            bank_x, bank_h, bank_y = psum[0:2], [psum[2:4], psum[4:6]], psum[6:8]

            def part_of(n, s):
                which, e = STAGED[n][1]
                w, parts = (w1, DC) if which == 0 else (w2, HC)
                return w[s][:, e * SPAN:(e + 1) * SPAN].rearrange("p (c n) -> p c n", c=parts)

            def splitter(n):
                by_pool = [m for m in range(len(STAGED)) if m % 3 == 1]
                if n in by_pool:
                    return "pool", by_pool.index(n) + 1
                return "dve", n + 1 - len([m for m in by_pool if m < n])

            def wait_split(engine, n):
                who, count = splitter(n)
                engine.wait_ge(stage_lo[who], count)

            stage_hi, stage_lo = sem("stage_hi"), {"dve": sem("stage_lo_dve"), "pool": sem("stage_lo_pool")}
            bias_in, bias_full, bias_done = sem("bias_in"), sem("bias_full"), sem("bias_done")
            table, numbered, padded = sem("table"), sem("numbered"), sem("padded")
            x_tile = [sem(f"x_tile{n}") for n in range(STEPS)]
            x_full, x_hi, x_lo, tagged = sem("x_full"), sem("x_hi"), sem("x_lo"), sem("tagged")
            w_set = sem("w_set")
            h_full, h_relu, h_hi, h_lo = sem("h_full"), sem("h_relu"), sem("h_hi"), sem("h_lo")
            y_full, y_biased, y_weighted, added = sem("y_full"), sem("y_biased"), sem("y_weighted"), sem("added")

            def due(engine, s, value):
                if not isinstance(value, int) or value > 0:
                    engine.wait_ge(s, value)

            def tiles(engine, body):
                body(0, False)
                with engine.Fori(1, TILES // STEPS - 1) as it:
                    body(it * STEPS, False)
                body(TILES - STEPS, True)

            block = stack.enter_context(nc.Block())

            @block.sync
            def _(sp):
                sp.dma_start(b1_rows[:, :], b1.rearrange("e (c p) -> (e c) p", p=P)).then_inc(bias_in, 16)
                sp.dma_start(b2_all[:, :], b2.rearrange("e d -> (e d)").rearrange("(o n) -> o n", o=1)
                             .to_broadcast([P, E * D])).then_inc(bias_in, 16)
                sp.wait_ge(table, 1)
                for e in range(E):
                    end = sp.value_load(end_of[0:1, e:e + 1], min_val=e * REGION, max_val=e * REGION + tokens)
                    sp.dma_start(lists[bass.ds(end, TILE), :].rearrange("(b p) d -> p b d", p=P),
                                 pad[:, :, :]).then_inc(padded, 16)
                sp.wait_ge(padded, 16 * E)
                sp.wait_ge(table, 18)
                for n in range(len(STAGED)):
                    if n + RAWS >= len(STAGED) and n % RAWS in (1, 2, 3):
                        wait_split(sp, n)

                def body(j0, last):
                    for u in range(STEPS):
                        j = j0 + u
                        due(sp, x_full, j + 1 - STEPS)
                        due(sp, tagged, j + 1 - STEPS)
                        row = sp.value_load(row_of[0:1, bass.ds(j, 1)], min_val=0, max_val=E * REGION)
                        sp.dma_start(xs[:, u, :, :], lists[bass.ds(row, TILE), :].rearrange("(b p) d -> p b d", p=P)
                                     ).then_inc(x_tile[u], 16)

                tiles(sp, body)

            @block.gpsimd
            def _(pool):
                pool.iota(tile_no[:, :], [[1, TILES]], base=0, channel_multiplier=0,
                          allow_small_or_imprecise_dtypes=True).then_inc(numbered, 1)
                for n in range(len(STAGED)):
                    if splitter(n)[0] == "pool":
                        pool.wait_ge(stage_hi, n + 1)
                        pool.tensor_tensor(part_of(n, 1), staged(n, STAGED[n][2]), part_of(n, 0).bitcast(F32),
                                           ALU.subtract).then_inc(stage_lo["pool"], 1)

                def weigh(j, u):
                    pool.wait_ge(y_biased, j + 1)
                    due(pool, y_weighted, 2 * j)
                    due(pool, added, (j - 1) * 32)
                    for b in range(2):
                        pool.tensor_tensor(yout[:, u % 2, b, :], ysum[:, u % 2, b, :],
                                           tag[:, u, b:b + 1].to_broadcast([P, D]), ALU.mult).then_inc(y_weighted, 1)

                def add(u):
                    for b in range(2):
                        pool.indirect_dma_start(out, bass.IndirectOffsetOnAxis(ap=number[:, u, b:b + 1], axis=0),
                                                yout[:, u % 2, b, :], None, compute_op=ALU.add).then_inc(added, 16)

                def body(j0, last):
                    for u in range(STEPS):
                        weigh(j0 + u, u)
                        if u > 0 or not isinstance(j0, int) or j0 > 0:
                            add((u - 1) % STEPS)

                tiles(pool, body)
                pool.wait_ge(y_weighted, 2 * TILES)
                pool.wait_ge(added, 32 * (TILES - 1))
                add(STEPS - 1)
                pool.wait_ge(added, 32 * TILES)

            @block.scalar
            def _(act):
                for n, (_, _, parts) in enumerate(STAGED):
                    act.wait_ge(stage_in[n % RAWS], 16 * (n // RAWS + 1))
                    act.activation(part_of(n, 0), staged(n, parts), ACT.Copy).then_inc(stage_hi, 1)
                    m = n + RAWS - 2
                    if RAWS <= m < len(STAGED):
                        wait_split(act, n - 2)
                        act.dma_start(staged(m, STAGED[m][2]), STAGED[m][0]).then_inc(stage_in[m % RAWS], 16)

                def x_part(j, u):
                    act.wait_ge(x_full, j + 1)
                    act.activation(xst[0][:, u % 2, :, :], bank_x[u % 2][:, :].rearrange("p (c t) -> p c t", c=DC),
                                   ACT.Copy).then_inc(x_hi, 1)

                def set_weights(j, u):
                    e = act.value_load(weights_of[0:1, bass.ds(j, 1)], min_val=0, max_val=(E - 1) * SPAN)
                    for s in range(2):
                        act.activation(wst[s][u % 2], w1[s][:, bass.ds(e, SPAN)].bitcast(F32), ACT.Copy)
                    act.activation(bst[:, u % 2, :], b1t[:, bass.ds(e // (SPAN // HC), HC)], ACT.Copy).then_inc(w_set, 1)

                def h_part(j, u, half):
                    act.wait_ge(h_relu, 2 * j + 1 + half)
                    at = slice(half * HC // 2, (half + 1) * HC // 2)
                    act.activation(hidt[0][:, u % 2, at, :], hid[:, at, :], ACT.Copy).then_inc(h_hi, 1)

                for n in range(len(STAGED) - RAWS, len(STAGED)):
                    wait_split(act, n)
                act.wait_ge(bias_done, 1)
                act.wait_ge(table, 18)

                def body(j0, last):
                    if isinstance(j0, int) and j0 == 0:
                        for u in range(2):
                            x_part(u, u)
                            set_weights(u, u)
                    for u in range(STEPS):
                        h_part(j0 + u, u, 0)
                        h_part(j0 + u, u, 1)
                        if not last or u < STEPS - 2:
                            x_part(j0 + u + 2, u)
                            set_weights(j0 + u + 2, u)

                tiles(act, body)

            @block.vector
            def _(dve):
                def split(first, last):
                    for n in range(first, last):
                        if splitter(n)[0] == "dve":
                            dve.wait_ge(stage_hi, n + 1)
                            dve.tensor_tensor(part_of(n, 1), staged(n, STAGED[n][2]), part_of(n, 0).bitcast(F32),
                                              ALU.subtract).then_inc(stage_lo["dve"], 1)

                split(0, RAWS)
                t = iter(range(2, 99))

                def next_step(instruction):
                    instruction.then_inc(table, 1)
                    dve.wait_ge(table, next(t))

                dve.tensor_copy(end_of[:, :], run[0:1, :]).then_inc(table, 1)
                next_step(dve.tensor_tensor(count[:, :], run[0:1, :], region0[0:1, :], ALU.subtract))
                next_step(dve.tensor_scalar(up_i[:, :], count[:, :], float(TILE - 1), None, ALU.add))
                next_step(dve.tensor_scalar(tiles_i[:, :], up_i[:, :], TILE.bit_length() - 1, None,
                                            ALU.arith_shift_right))
                next_step(dve.tensor_copy(tiles_f[:, :], tiles_i[:, :]))
                next_step(dve.tensor_tensor(ahead_m[:, :, :], before[0:1, :, :],
                                            tiles_f[:, :].rearrange("p (o f) -> p o f", o=1).to_broadcast([1, E, E]),
                                            ALU.mult))
                next_step(dve.tensor_reduce(ahead[:, :], ahead_m[:, :, :], AX.X, ALU.add))
                next_step(dve.tensor_tensor(upto[:, :], ahead[:, :], tiles_f[:, :], ALU.add))
                next_step(dve.tensor_scalar(jump[:, :], tiles_f[:, :], -float(TILE), float(REGION), ALU.mult, ALU.add))
                dve.wait_ge(numbered, 1)
                per_tile = lambda v: v.rearrange("p (o e) -> p o e", o=1).to_broadcast([1, TILES, E])
                next_step(dve.tensor_tensor(past[:, :, :], tile_no[:, :].rearrange("p (j o) -> p j o", o=1)
                                            .to_broadcast([1, TILES, E]), per_tile(upto[:, :]), ALU.is_ge))
                next_step(dve.tensor_reduce(expert_f[:, :], past[:, :, :], AX.X, ALU.add))
                next_step(dve.tensor_scalar(expert_of[:, :], expert_f[:, :], float(E - 1), None, ALU.min))
                next_step(dve.tensor_scalar(weights_of[:, :], expert_f[:, :], float(E - 1), float(SPAN),
                                            ALU.min, ALU.mult))
                next_step(dve.tensor_tensor(past[:, :, :], past[:, :, :], per_tile(jump[:, :]), ALU.mult))
                next_step(dve.tensor_reduce(offset_f[:, :], past[:, :, :], AX.X, ALU.add))
                next_step(dve.scalar_tensor_tensor(row_f[:, :], tile_no[:, :], float(TILE), offset_f[:, :],
                                                   ALU.mult, ALU.add))
                next_step(dve.tensor_scalar(row_c[:, :], row_f[:, :], float(E * REGION), None, ALU.min))
                dve.tensor_copy(row_of[:, :], row_c[:, :]).then_inc(table, 1)

                split(RAWS, len(STAGED))

                dve.wait_ge(bias_full, 1)
                dve.tensor_copy(b1t[:, :], bank_y[0][:, 0:E * HC]).then_inc(bias_done, 1)

                def x_part(j, u):
                    dve.wait_ge(x_hi, j + 1)
                    dve.tensor_tensor(xst[1][:, u % 2, :, :], bank_x[u % 2][:, :].rearrange("p (c t) -> p c t", c=DC),
                                      xst[0][:, u % 2, :, :].bitcast(F32), ALU.subtract).then_inc(x_lo, 1)

                def tags(j, u):
                    due(dve, added, (j + 1 - STEPS) * 32)
                    dve.wait_ge(x_full, j + 1)
                    dve.tensor_copy(tag[:, u, :], xs[:, u, :, D])
                    dve.tensor_copy(number[:, u, :], xs[:, u, :, D + 1]).then_inc(tagged, 1)

                def relu(j, u, half):
                    dve.wait_ge(h_full, 2 * j + 1 + half)
                    due(dve, h_lo, 2 * j - 1 + half)
                    for k in range(2):
                        c = 2 * half + k
                        last = dve.tensor_scalar(hid[:, c, :], bank_h[u % 2][half][:, k * TILE:(k + 1) * TILE],
                                                 bst[:, u % 2, c:c + 1], 0.0, ALU.add, ALU.max)
                    last.then_inc(h_relu, 1)

                def h_part(j, u, half):
                    dve.wait_ge(h_hi, 2 * j + 1 + half)
                    at = slice(half * HC // 2, (half + 1) * HC // 2)
                    dve.tensor_tensor(hidt[1][:, u % 2, at, :], hid[:, at, :], hidt[0][:, u % 2, at, :].bitcast(F32),
                                      ALU.subtract).then_inc(h_lo, 1)

                def bias2(j, u):
                    e = dve.value_load(expert_of[0:1, bass.ds(j, 1)], min_val=0, max_val=E - 1)
                    dve.wait_ge(y_full, j + 1)
                    due(dve, y_weighted, 2 * (j - 1))
                    for b in range(2):
                        last = dve.tensor_tensor(ysum[:, u % 2, b, :], bank_y[u % 2][:, b * D:(b + 1) * D],
                                                 b2_all[:, bass.ds(e * D, D)], ALU.add)
                    last.then_inc(y_biased, 1)

                dve.wait_ge(bias_in, 32)
                for n in range(len(STAGED) - 3, len(STAGED)):
                    wait_split(dve, n)

                def body(j0, last):
                    if isinstance(j0, int) and j0 == 0:
                        x_part(0, 0)
                        x_part(1, 1)
                    for u in range(STEPS):
                        relu(j0 + u, u, 0)
                        relu(j0 + u, u, 1)
                        h_part(j0 + u, u, 0)
                        h_part(j0 + u, u, 1)
                        if not last or u < STEPS - 2:
                            x_part(j0 + u + 2, u)
                        tags(j0 + u, u)
                        if u > 0 or not isinstance(j0, int) or j0 > 0:
                            bias2(j0 + u - 1, (u - 1) % 2)

                tiles(dve, body)
                bias2(TILES - 1, 1)

            @block.tensor
            def _(pe):
                def three(dst, stat, move, start, stop):
                    for m, (s, r) in enumerate(((0, 1), (1, 0), (0, 0))):
                        last = pe.matmul(dst, stat[s], move[r], start=start and m == 0, stop=stop and m == 2)
                    return last

                def turn_x(j, u):
                    if isinstance(j, int):
                        pe.wait_ge(x_tile[u], 16 * (j // STEPS + 1))
                    else:
                        pe.wait_ge(x_tile[u], (j - u) * (16 // STEPS) + 16)
                    for c in range(DC):
                        for b in range(2):
                            last = pe.transpose(bank_x[u % 2][:, (2 * c + b) * P:(2 * c + b + 1) * P],
                                                xs[:, u, b, c * P:(c + 1) * P], ident[:, :])
                    last.then_inc(x_full, 1)

                def up(j, u):
                    pe.wait_ge(x_lo, j + 1)
                    pe.wait_ge(w_set, j + 1)
                    for hc in range(HC):
                        for c in range(DC):
                            last = three(bank_h[u % 2][hc // 2][:, (hc % 2) * TILE:(hc % 2 + 1) * TILE],
                                         [wst[s][u % 2][:, c * H + hc * P:c * H + (hc + 1) * P] for s in range(2)],
                                         [xst[s][:, u % 2, c, :] for s in range(2)], c == 0, c == DC - 1)
                        if hc % 2:
                            last.then_inc(h_full, 1)

                def down(j, u):
                    e = pe.value_load(weights_of[0:1, bass.ds(j, 1)], min_val=0, max_val=(E - 1) * SPAN)
                    pe.wait_ge(h_lo, 2 * (j + 1))
                    for b in range(2):
                        for c in range(HC):
                            last = three(bank_y[u % 2][:, b * D:(b + 1) * D],
                                         [hidt[s][:, u % 2, c, b * P:(b + 1) * P] for s in range(2)],
                                         [w2[s][:, bass.ds(e + c * D, D)] for s in range(2)], c == 0, c == HC - 1)
                    last.then_inc(y_full, 1)

                def body(j0, last):
                    if isinstance(j0, int) and j0 == 0:
                        turn_x(0, 0)
                        turn_x(1, 1)
                        up(0, 0)
                    for u in range(STEPS):
                        if not last or u < STEPS - 2:
                            turn_x(j0 + u + 2, (u + 2) % STEPS)
                        if not last or u < STEPS - 1:
                            up(j0 + u + 1, (u + 1) % STEPS)
                        down(j0 + u, u)

                pe.wait_ge(bias_in, 32)
                pe.transpose(bank_y[0][:, 0:E * HC], b1_rows[:, :], ident[0:E * HC, 0:E * HC]).then_inc(bias_full, 1)
                pe.wait_ge(table, 18)
                for n in range(len(STAGED) - 3, len(STAGED)):
                    wait_split(pe, n)
                tiles(pe, body)


def kernel(x, ctx_768, L0_xattn_w_q, L0_xattn_w_k, L0_xattn_w_v, L0_xattn_w_o, L0_xattn_b_o, L0_ffn_gate,
           L0_ffn_W1, L0_ffn_b1, L0_ffn_W2, L0_ffn_b2):
    import concourse.bacc as bacc
    from concourse.bass_utils import run_bass_kernel_spmd

    nc = bacc.Bacc("TRN2", target_bir_lowering=False, num_devices=1)
    B, S, D = x.shape
    given = {
        "x": np.ascontiguousarray(x).reshape(B * S, D),
        "ctx": np.ascontiguousarray(ctx_768).reshape(B * S, -1),
        "w_q": L0_xattn_w_q, "w_k": L0_xattn_w_k, "w_v": L0_xattn_w_v, "w_o": L0_xattn_w_o, "b_o": L0_xattn_b_o,
        "gate": L0_ffn_gate, "W1": L0_ffn_W1, "b1": L0_ffn_b1, "W2": L0_ffn_W2, "b2": L0_ffn_b2,
    }
    arrays = {f"in_{k}": np.ascontiguousarray(v) for k, v in given.items()}
    aps = [nc.dram_tensor(k, a.shape, mybir.dt.from_np(a.dtype), kind="ExternalInput").ap() for k, a in arrays.items()]
    out = nc.dram_tensor("out", (B * S + 2 * P, D), F32, kind="ExternalOutput").ap()
    program(nc, *aps, out)
    r = run_bass_kernel_spmd(nc, [arrays], core_ids=[0])
    return r.results[0]["out"][:B * S].reshape(B, S, D)
```
